# Optimizing a Trainium2 kernel written in Bass

```python
import numpy as np
import jax
import jax.numpy as jnp

def _softmax(x, axis=-1):
    return jax.nn.softmax(x, axis=axis)

def _gelu(x):
    return jax.nn.gelu(x, approximate=True)

def _silu(x):
    return jax.nn.silu(x)

def _sigmoid(x):
    return jax.nn.sigmoid(x)

def _layernorm(x, axis=-1, eps=1e-05):
    m = jnp.mean(x, axis=axis, keepdims=True)
    v = jnp.var(x, axis=axis, keepdims=True)
    return (x - m) / jnp.sqrt(v + eps)

def _scatter_add(tgt, idx, src, axis=0):
    return tgt.at[idx].add(src)

def _segment_sum(src, seg, n):
    return jax.ops.segment_sum(src, seg, n)
kernel_name = 'mk_sandwich_d2_jaxref_r8_994ced'

def setup_inputs(seed: int=0):
    np.random.seed(seed)
    _w = jnp.asarray

    def _L0_attn_setup():
        import jax, jax.numpy as jnp
        import numpy as np
        from jax import lax
        D_MODEL = 128
        B, T = (4, 256)
        LN_EPS = 1e-05

        def _ln(x, w, b):
            mu = jnp.mean(x, axis=-1, keepdims=True)
            var = jnp.mean((x - mu) ** 2, axis=-1, keepdims=True)
            return (x - mu) * lax.rsqrt(var + LN_EPS) * w + b

        def _wkv(u, k, v):
            Bb, Tt, C = k.shape

            def step(carry, kv):
                aa, bb = carry
                kk, vv = kv
                p = jnp.maximum(bb, u + kk)
                e1 = jnp.exp(bb - p)
                e2 = jnp.exp(u + kk - p)
                out = (e1 * aa + e2 * vv) / (e1 + e2)
                p2 = jnp.maximum(bb, kk)
                e1b = jnp.exp(bb - p2)
                e2b = jnp.exp(kk - p2)
                return ((e1b * aa + e2b * vv, p2 + jnp.log(e1b + e2b)), out)
            init = (jnp.zeros((Bb, C), k.dtype), jnp.zeros((Bb, C), k.dtype))
            _, outs = lax.scan(step, init, (jnp.swapaxes(k, 0, 1), jnp.swapaxes(v, 0, 1)))
            return jnp.swapaxes(outs, 0, 1)
        key = jax.random.key(seed)
        ks = jax.random.split(key, 12)
        C = D_MODEL
        s = 0.02
        return {'x': jax.random.normal(ks[0], (B, T, C), jnp.float32), 'time_decay': jax.random.normal(ks[1], (C,), jnp.float32), 'time_first': jax.random.normal(ks[2], (C,), jnp.float32) * 0.5, 'time_shift': jax.random.normal(ks[3], (1, 1, C), jnp.float32) * 0.1, 'Wk': jax.random.normal(ks[4], (C, C), jnp.float32) * s, 'Wv': jax.random.normal(ks[5], (C, C), jnp.float32) * s, 'Wr': jax.random.normal(ks[6], (C, C), jnp.float32) * s, 'Wck': jax.random.normal(ks[7], (4 * C, C), jnp.float32) * s, 'Wcv': jax.random.normal(ks[8], (C, 4 * C), jnp.float32) * s, 'Wcr': jax.random.normal(ks[9], (C, C), jnp.float32) * s, 'ln1_w': jnp.ones((C,), jnp.float32), 'ln1_b': jnp.zeros((C,), jnp.float32), 'ln2_w': jnp.ones((C,), jnp.float32), 'ln2_b': jnp.zeros((C,), jnp.float32)}
    _L0_attn_in = _L0_attn_setup()

    def _L0_ffn_setup():
        import jax, jax.numpy as jnp
        import numpy as np
        D_IN, D_HID = (128, 512)

        def _ternary(key, shape):
            return jax.random.randint(key, shape, -1, 2).astype(jnp.float32)

        def _tlin(x, w, s):
            return jnp.einsum('bsi,oi->bso', x, w) * s
        key = jax.random.key(seed)
        ks = jax.random.split(key, 12)
        inv = lambda fan: 1.0 / np.sqrt(fan).astype(np.float32)
        return {'x': jax.random.normal(ks[0], (4, 256, D_IN), dtype=jnp.float32), 'w1_w': _ternary(ks[1], (D_HID, D_IN)), 'w1_s': jax.random.uniform(ks[2], (D_HID,), dtype=jnp.float32) * inv(D_IN), 'w2_w': _ternary(ks[3], (D_HID, D_IN)), 'w2_s': jax.random.uniform(ks[4], (D_HID,), dtype=jnp.float32) * inv(D_IN), 'h1_w': _ternary(ks[5], (D_HID, D_HID)), 'h1_s': jax.random.uniform(ks[6], (D_HID,), dtype=jnp.float32) * inv(D_HID), 'h2_w': _ternary(ks[7], (D_HID, D_HID)), 'h2_s': jax.random.uniform(ks[8], (D_HID,), dtype=jnp.float32) * inv(D_HID), 'w3_w': _ternary(ks[9], (D_IN, D_HID)), 'w3_s': jax.random.uniform(ks[10], (D_IN,), dtype=jnp.float32) * inv(D_HID)}
    _L0_ffn_in = _L0_ffn_setup()

    def _L1_attn_setup():
        import jax, jax.numpy as jnp
        import numpy as np
        B, S, H = (1, 256, 128)
        INTER, K, DST, DTR = (256, 4, 16, 64)

        def _ssm(dA, dBu, C):
            xs = (jnp.moveaxis(dA, 1, 0), jnp.moveaxis(dBu, 1, 0), jnp.moveaxis(C, 1, 0))
            state0 = jnp.zeros(dA.shape[:1] + dA.shape[2:], dA.dtype)

            def step(state, inp):
                Ai, dBui, Ci = inp
                state = Ai * state + dBui
                y = jnp.einsum('bhd,bd->bh', state, Ci)
                return (state, y)
            _, ys = jax.lax.scan(step, state0, xs)
            return jnp.moveaxis(ys, 0, 1)
        key = jax.random.key(seed)
        ks = jax.random.split(key, 10)
        sc = 0.02
        return {'x': jax.random.normal(ks[0], (B, S, H), jnp.float32), 'W_in': jax.random.normal(ks[1], (H, 2 * INTER), jnp.float32) * sc, 'conv_w': jax.random.normal(ks[2], (K, 1, INTER), jnp.float32) * sc, 'conv_b': jax.random.normal(ks[3], (INTER,), jnp.float32) * sc, 'W_x': jax.random.normal(ks[4], (INTER, DTR + 2 * DST), jnp.float32) * sc, 'W_dt': jax.random.normal(ks[5], (DTR, INTER), jnp.float32) * sc, 'b_dt': jax.random.normal(ks[6], (INTER,), jnp.float32) * sc, 'A_log': jax.random.normal(ks[7], (INTER, DST), jnp.float32) * sc, 'D': jax.random.normal(ks[8], (INTER,), jnp.float32) * sc, 'W_out': jax.random.normal(ks[9], (INTER, H), jnp.float32) * sc}
    _L1_attn_in = _L1_attn_setup()

    def _L1_ffn_setup():
        import jax, jax.numpy as jnp
        import numpy as np
        HIDDEN = 128
        FFN = 512
        NUM_EXPERTS = 8
        TOP_K = 2
        BATCH, SEQ = (2, 256)
        key = jax.random.key(seed)
        ks = jax.random.split(key, 6)
        s_h = 1.0 / np.sqrt(HIDDEN)
        s_f = 1.0 / np.sqrt(FFN)
        return {'hidden_states': jax.random.normal(ks[0], (BATCH, SEQ, HIDDEN), jnp.float32), 'gate_w': jax.random.uniform(ks[1], (HIDDEN, NUM_EXPERTS), jnp.float32, -s_h, s_h), 'gate_b': jax.random.uniform(ks[2], (NUM_EXPERTS,), jnp.float32, -s_h, s_h), 'w1': jax.random.uniform(ks[3], (NUM_EXPERTS, HIDDEN, FFN), jnp.float32, -s_h, s_h), 'w3': jax.random.uniform(ks[4], (NUM_EXPERTS, HIDDEN, FFN), jnp.float32, -s_h, s_h), 'w2': jax.random.uniform(ks[5], (NUM_EXPERTS, FFN, HIDDEN), jnp.float32, -s_f, s_f)}
    _L1_ffn_in = _L1_ffn_setup()
    _d = {'L0_attn_x': _L0_attn_in['x'], 'L0_attn_time_decay': _L0_attn_in['time_decay'], 'L0_attn_time_first': _L0_attn_in['time_first'], 'L0_attn_time_shift': _L0_attn_in['time_shift'], 'L0_attn_Wk': _L0_attn_in['Wk'], 'L0_attn_Wv': _L0_attn_in['Wv'], 'L0_attn_Wr': _L0_attn_in['Wr'], 'L0_attn_Wck': _L0_attn_in['Wck'], 'L0_attn_Wcv': _L0_attn_in['Wcv'], 'L0_attn_Wcr': _L0_attn_in['Wcr'], 'L0_attn_ln1_w': _L0_attn_in['ln1_w'], 'L0_attn_ln1_b': _L0_attn_in['ln1_b'], 'L0_attn_ln2_w': _L0_attn_in['ln2_w'], 'L0_attn_ln2_b': _L0_attn_in['ln2_b'], 'L0_ffn_w1_w': _L0_ffn_in['w1_w'], 'L0_ffn_w1_s': _L0_ffn_in['w1_s'], 'L0_ffn_w2_w': _L0_ffn_in['w2_w'], 'L0_ffn_w2_s': _L0_ffn_in['w2_s'], 'L0_ffn_h1_w': _L0_ffn_in['h1_w'], 'L0_ffn_h1_s': _L0_ffn_in['h1_s'], 'L0_ffn_h2_w': _L0_ffn_in['h2_w'], 'L0_ffn_h2_s': _L0_ffn_in['h2_s'], 'L0_ffn_w3_w': _L0_ffn_in['w3_w'], 'L0_ffn_w3_s': _L0_ffn_in['w3_s'], 'L1_attn_W_in': _L1_attn_in['W_in'], 'L1_attn_conv_w': _L1_attn_in['conv_w'], 'L1_attn_conv_b': _L1_attn_in['conv_b'], 'L1_attn_W_x': _L1_attn_in['W_x'], 'L1_attn_W_dt': _L1_attn_in['W_dt'], 'L1_attn_b_dt': _L1_attn_in['b_dt'], 'L1_attn_A_log': _L1_attn_in['A_log'], 'L1_attn_D': _L1_attn_in['D'], 'L1_attn_W_out': _L1_attn_in['W_out'], 'L1_ffn_gate_w': _L1_ffn_in['gate_w'], 'L1_ffn_gate_b': _L1_ffn_in['gate_b'], 'L1_ffn_w1': _L1_ffn_in['w1'], 'L1_ffn_w3': _L1_ffn_in['w3'], 'L1_ffn_w2': _L1_ffn_in['w2']}
    _x0 = _d['L0_attn_x']
    _d['L0_attn_x'] = jax.random.normal(jax.random.fold_in(jax.random.key(seed), 1), (2, 2048, 128), dtype=_x0.dtype)
    del _x0
    return _d

def reference(L0_attn_x, L0_attn_time_decay, L0_attn_time_first, L0_attn_time_shift, L0_attn_Wk, L0_attn_Wv, L0_attn_Wr, L0_attn_Wck, L0_attn_Wcv, L0_attn_Wcr, L0_attn_ln1_w, L0_attn_ln1_b, L0_attn_ln2_w, L0_attn_ln2_b, L0_ffn_w1_w, L0_ffn_w1_s, L0_ffn_w2_w, L0_ffn_w2_s, L0_ffn_h1_w, L0_ffn_h1_s, L0_ffn_h2_w, L0_ffn_h2_s, L0_ffn_w3_w, L0_ffn_w3_s, L1_attn_W_in, L1_attn_conv_w, L1_attn_conv_b, L1_attn_W_x, L1_attn_W_dt, L1_attn_b_dt, L1_attn_A_log, L1_attn_D, L1_attn_W_out, L1_ffn_gate_w, L1_ffn_gate_b, L1_ffn_w1, L1_ffn_w3, L1_ffn_w2):

    def _L0_attn_ref(x, time_decay, time_first, time_shift, Wk, Wv, Wr, Wck, Wcv, Wcr, ln1_w, ln1_b, ln2_w, ln2_b):
        import jax, jax.numpy as jnp
        import numpy as np
        from jax import lax
        D_MODEL = 128
        B, T = (4, 256)
        LN_EPS = 1e-05

        def _ln(x, w, b):
            mu = jnp.mean(x, axis=-1, keepdims=True)
            var = jnp.mean((x - mu) ** 2, axis=-1, keepdims=True)
            return (x - mu) * lax.rsqrt(var + LN_EPS) * w + b

        def _wkv(u, k, v):
            Bb, Tt, C = k.shape

            def step(carry, kv):
                aa, bb = carry
                kk, vv = kv
                p = jnp.maximum(bb, u + kk)
                e1 = jnp.exp(bb - p)
                e2 = jnp.exp(u + kk - p)
                out = (e1 * aa + e2 * vv) / (e1 + e2)
                p2 = jnp.maximum(bb, kk)
                e1b = jnp.exp(bb - p2)
                e2b = jnp.exp(kk - p2)
                return ((e1b * aa + e2b * vv, p2 + jnp.log(e1b + e2b)), out)
            init = (jnp.zeros((Bb, C), k.dtype), jnp.zeros((Bb, C), k.dtype))
            _, outs = lax.scan(step, init, (jnp.swapaxes(k, 0, 1), jnp.swapaxes(v, 0, 1)))
            return jnp.swapaxes(outs, 0, 1)
        Bb, Tt, C = x.shape
        ts = time_shift
        h = _ln(x, ln1_w, ln1_b)
        x_shifted = jnp.concatenate([jnp.broadcast_to(ts, (Bb, 1, C)), h[:, :-1, :]], axis=1)
        xxx = h + (h - x_shifted) * ts
        k = jnp.einsum('btc,oc->bto', xxx, Wk)
        v = jnp.einsum('btc,oc->bto', xxx, Wv)
        r = jax.nn.sigmoid(jnp.einsum('btc,oc->bto', xxx, Wr))
        wkv = _wkv(time_first, k, v)
        x = x + r * wkv
        h2 = _ln(x, ln2_w, ln2_b)
        xx2 = jnp.concatenate([h2[:, -1:, :], h2[:, :-1, :]], axis=1)
        xxx2 = h2 + (xx2 - h2) * ts
        kc = jnp.einsum('btc,oc->bto', xxx2, Wck)
        rc = jax.nn.sigmoid(jnp.einsum('btc,oc->bto', xxx2, Wcr))
        vv = jnp.einsum('bth,ch->btc', jax.nn.relu(kc) ** 2, Wcv)
        return x + rc * vv

    def _L0_ffn_ref(x, w1_w, w1_s, w2_w, w2_s, h1_w, h1_s, h2_w, h2_s, w3_w, w3_s):
        import jax, jax.numpy as jnp
        import numpy as np
        D_IN, D_HID = (128, 512)

        def _ternary(key, shape):
            return jax.random.randint(key, shape, -1, 2).astype(jnp.float32)

        def _tlin(x, w, s):
            return jnp.einsum('bsi,oi->bso', x, w) * s
        h = jax.nn.silu(_tlin(x, w1_w, w1_s)) * _tlin(x, w2_w, w2_s)
        h = jax.nn.gelu(_tlin(h, h1_w, h1_s), approximate=False)
        h = jax.nn.gelu(_tlin(h, h2_w, h2_s), approximate=False)
        return _tlin(h, w3_w, w3_s)

    def _L1_attn_ref(x, W_in, conv_w, conv_b, W_x, W_dt, b_dt, A_log, D, W_out):
        import jax, jax.numpy as jnp
        import numpy as np
        B, S, H = (1, 256, 128)
        INTER, K, DST, DTR = (256, 4, 16, 64)

        def _ssm(dA, dBu, C):
            xs = (jnp.moveaxis(dA, 1, 0), jnp.moveaxis(dBu, 1, 0), jnp.moveaxis(C, 1, 0))
            state0 = jnp.zeros(dA.shape[:1] + dA.shape[2:], dA.dtype)

            def step(state, inp):
                Ai, dBui, Ci = inp
                state = Ai * state + dBui
                y = jnp.einsum('bhd,bd->bh', state, Ci)
                return (state, y)
            _, ys = jax.lax.scan(step, state0, xs)
            return jnp.moveaxis(ys, 0, 1)
        proj = x @ W_in
        raw, gate = jnp.split(proj, 2, axis=-1)
        conv = jax.lax.conv_general_dilated(raw, conv_w, window_strides=(1,), padding=[(K - 1, 0)], dimension_numbers=('NWC', 'WIO', 'NWC'), feature_group_count=INTER)
        h = jax.nn.silu(conv + conv_b)
        ssm_p = h @ W_x
        ts, Bmat, C = jnp.split(ssm_p, [DTR, DTR + DST], axis=-1)
        dt = jax.nn.softplus(ts @ W_dt + b_dt)
        A = -jnp.exp(A_log)
        dA = jnp.exp(dt[..., None] * A)
        dBu = dt[..., None] * Bmat[:, :, None, :] * h[..., None]
        y = _ssm(dA, dBu, C)
        y = y + h * D
        y = y * jax.nn.silu(gate)
        return y @ W_out

    def _L1_ffn_ref(hidden_states, gate_w, gate_b, w1, w3, w2):
        import jax, jax.numpy as jnp
        import numpy as np
        HIDDEN = 128
        FFN = 512
        NUM_EXPERTS = 8
        TOP_K = 2
        BATCH, SEQ = (2, 256)
        B, S, D = hidden_states.shape
        T = B * S
        x = hidden_states.reshape(T, D)
        logits = x @ gate_w + gate_b
        probs = jax.nn.softmax(logits.astype(jnp.float32), axis=-1)
        top_w, top_idx = jax.lax.top_k(probs, TOP_K)
        top_w = top_w / jnp.sum(top_w, axis=-1, keepdims=True)
        combine = jnp.zeros((T, NUM_EXPERTS), jnp.float32)
        combine = combine.at[jnp.arange(T)[:, None], top_idx].set(top_w)
        combine = combine.astype(x.dtype)
        h = jax.nn.silu(jnp.einsum('td,edf->tef', x, w1)) * jnp.einsum('td,edf->tef', x, w3)
        out_e = jnp.einsum('tef,efd->ted', h, w2)
        out = jnp.einsum('ted,te->td', out_e, combine)
        return out.reshape(B, S, D)
    x = L0_attn_x
    x = x + _layernorm(_L0_attn_ref(_layernorm(x, axis=-1), L0_attn_time_decay, L0_attn_time_first, L0_attn_time_shift, L0_attn_Wk, L0_attn_Wv, L0_attn_Wr, L0_attn_Wck, L0_attn_Wcv, L0_attn_Wcr, L0_attn_ln1_w, L0_attn_ln1_b, L0_attn_ln2_w, L0_attn_ln2_b), axis=-1)
    x = x + _layernorm(_L0_ffn_ref(_layernorm(x, axis=-1), L0_ffn_w1_w, L0_ffn_w1_s, L0_ffn_w2_w, L0_ffn_w2_s, L0_ffn_h1_w, L0_ffn_h1_s, L0_ffn_h2_w, L0_ffn_h2_s, L0_ffn_w3_w, L0_ffn_w3_s), axis=-1)
    x = x + _layernorm(_L1_attn_ref(_layernorm(x, axis=-1), L1_attn_W_in, L1_attn_conv_w, L1_attn_conv_b, L1_attn_W_x, L1_attn_W_dt, L1_attn_b_dt, L1_attn_A_log, L1_attn_D, L1_attn_W_out), axis=-1)
    x = x + _layernorm(_L1_ffn_ref(_layernorm(x, axis=-1), L1_ffn_gate_w, L1_ffn_gate_b, L1_ffn_w1, L1_ffn_w3, L1_ffn_w2), axis=-1)
    return x

_drawn_inputs = setup_inputs


def setup_inputs(seed=0):
    import zlib

    import numpy as np

    out = dict(_drawn_inputs(seed))
    spreads = {'L0_attn_ln1_w': (1.0, 0.2),
     'L0_attn_ln1_b': (0.0, 0.1),
     'L0_attn_ln2_w': (1.0, 0.6),
     'L0_attn_ln2_b': (0.0, 0.529)}
    factors = {'L0_attn_time_first': 7.533,
     'L0_attn_Wcr': 5.275,
     'L1_attn_W_in': 4.553,
     'L1_attn_conv_w': 6.357,
     'L1_attn_conv_b': 4.697,
     'L1_attn_W_x': 8.0,
     'L1_attn_W_dt': 8.0,
     'L1_attn_b_dt': 8.0,
     'L1_attn_A_log': 8.0,
     'L1_attn_D': 4.685,
     'L1_attn_W_out': 5.554}
    for name, (base, spread) in spreads.items():
        noise = np.random.default_rng([zlib.crc32(name.encode()), seed]).standard_normal(out[name].shape)
        drawn = base * np.exp(spread * noise) if base else spread * noise
        out[name] = jnp.asarray(drawn.astype(out[name].dtype))
    for name, factor in factors.items():
        out[name] = (out[name] * factor).astype(out[name].dtype)
    return out
```

```python
from contextlib import ExitStack, contextmanager

import concourse.bass as bass
from concourse import mybir

F32 = mybir.dt.float32
BF16 = mybir.dt.bfloat16
ALU = mybir.AluOpType
ACT = mybir.ActivationFunctionType
AX = mybir.AxisListType

P = 128
B = 2
T = 2048
N = 512
NT = T // N
FFN = 512
FC = FFN // P
INTER = 256
CB = INTER // P
DST = 16
DTR = 64
TAPS = 4
E = 8
EPS = 1e-5

VECS = {}
NV = 0
for _name, _count in (
    ("time_first", 1), ("time_shift", 1), ("ln1_w", 1), ("ln1_b", 1), ("ln2_w", 1), ("ln2_b", 1),
    ("w1_s", FC), ("w2_s", FC), ("h1_s", FC), ("h2_s", FC), ("w3_s", 1),
    ("conv_w", TAPS * CB), ("conv_b", CB), ("b_dt", CB), ("D", CB), ("A_log", CB * DST), ("gate_b", E),
):
    VECS[_name] = NV
    NV += _count


def build(nc, xT, vecs, att_w, cv_w, tern_w, hid_w, w3_w, ssm_w, dt_w, moe_w13, moe_w2, gate_w, consts, selectors, iota_c, outT,
          last_phase=4):
    ctx = ExitStack()
    with ctx:
        def sb(name, shape, dt=F32, scope=ctx):
            return scope.enter_context(nc.sbuf_tensor(name, shape, dt))

        def sem(name):
            return ctx.enter_context(nc.semaphore(name))

        X = sb("X", [P, B, T])
        vec = sb("vec", [P, NV])
        const = sb("const", [P, 3, P])
        ident, centre, ones = const[:, 0, :], const[:, 1, :], const[:, 2, :]
        sel = sb("sel", [3 * 2 * DST, 2 * DST, P], BF16)
        ssmw = sb("ssmw", [P, 2 * INTER + CB * (DTR + 6 * DST) + CB * P])
        win = ssmw[:, 0:2 * INTER]
        wx = ssmw[:, 2 * INTER:2 * INTER + CB * (DTR + 6 * DST)].rearrange("p (c m) -> p c m", c=CB)
        wout = ssmw[:, 2 * INTER + CB * (DTR + 6 * DST):].rearrange("p (c m) -> p c m", c=CB)
        dtw = sb("dtw", [DTR, INTER])
        gatew = sb("gatew", [P, E])
        small = sb("small", [P, 8])
        eps_c, eps2_c, one_p_ts, one_m_ts, ts_m_b, zero_c = (small[:, i:i + 1] for i in range(6))

        def col(name, i=0):
            return vec[:, VECS[name] + i:VECS[name] + i + 1]

        att_loaded, ffn_loaded, ssm_loaded, moe_loaded = (
            sem(n) for n in ("att_loaded", "ffn_loaded", "ssm_loaded", "moe_loaded"))
        x_loaded = sem("x_loaded")
        smalls_ready = sem("smalls_ready")

        def ds(t, extra=0, size=N):
            return bass.ds(t * N + extra, size)

        with ExitStack() as mem12:
            XA = sb("XA", [P, B, T], scope=mem12)
            G2 = sb("G2", [P, B, T + 1], scope=mem12)
            attw = sb("attw", [P, 8, P], scope=mem12)
            cvw = sb("cvw", [P, FC, P], scope=mem12)
            ternw = sb("ternw", [P, 2, FFN], scope=mem12)
            hidw = sb("hidw", [P, 2, FC, FFN], scope=mem12)
            w3w = sb("w3w", [P, FFN], scope=mem12)
            G = Shared()
            G.X, G.XA, G.G2, G.vec, G.const, G.ident, G.centre = (
                X, XA, G2, vec, const, ident, centre)
            G.ones, G.sel, G.attw, G.cvw, G.ternw, G.hidw, G.w3w = (
                ones, sel, attw, cvw, ternw, hidw, w3w)
            G.ssmw, G.win, G.wx, G.wout, G.dtw, G.gatew, G.eps_c = (
                ssmw, win, wx, wout, dtw, gatew, eps_c)
            G.eps2_c, G.one_p_ts, G.one_m_ts, G.ts_m_b, G.zero_c, G.col, G.ds = (
                eps2_c, one_p_ts, one_m_ts, ts_m_b, zero_c, col, ds)
            G.x_loaded, G.att_loaded, G.ffn_loaded, G.ssm_loaded, G.moe_loaded, G.smalls_ready, G.xT = (
                x_loaded, att_loaded, ffn_loaded, ssm_loaded, moe_loaded, smalls_ready, xT)
            G.vecs, G.att_w, G.cv_w, G.tern_w, G.hid_w, G.w3_w, G.ssm_w = (
                vecs, att_w, cv_w, tern_w, hid_w, w3_w, ssm_w)
            G.dt_w, G.moe_w13, G.moe_w2, G.gate_w, G.consts, G.selectors, G.iota_c = (
                dt_w, moe_w13, moe_w2, gate_w, consts, selectors, iota_c)
            G.outT = (
                outT)
            phase_time_mix(nc, G)
            if last_phase == 1:
                return finish(nc, ctx, XA, outT)
            phase_ffn(nc, G)
        moe13 = sb("moe13", [P, E, 2 * FFN])
        moe2 = sb("moe2", [P, E * FC, P])
        G.moe13, G.moe2 = moe13, moe2
        if last_phase >= 3:
            phase_ssm(nc, G)
        if last_phase >= 4:
            phase_moe(nc, G)
        else:
            finish(nc, ctx, X, outT)


def finish(nc, ctx, src, outT):
    done = ctx.enter_context(nc.semaphore("out_done"))
    with nc.Block() as block:
        @block.sync
        def _(sp):
            sp.dma_start(outT, src[:, :, :]).then_inc(done, 16)
            sp.wait_ge(done, 16)


class Shared:
    pass


@contextmanager
def semaphores_of_phase(nc, prefix, names):
    sems = {n: nc.alloc_semaphore(name=prefix + n) for n in names}
    yield sems
    nc.clear_and_free_semaphores(list(sems.values()))
    nc.all_engine_barrier()


def phase_time_mix(nc, G):
    vec, X, XA, G2, col, ds = G.vec, G.X, G.XA, G.G2, G.col, G.ds
    mem = ExitStack()
    with mem:
        def sb(name, shape, dt=F32):
            return mem.enter_context(nc.sbuf_tensor(name, shape, dt))

        sq = sb("sq1", [P, B, N])
        lnv = sb("lnv1", [P, B, 2 * N])
        rstd = sb("rstd1", [P, B, 2 * N])
        xn = sb("xn1", [P, B, N])
        tsg = sb("tsg1", [P, B, N])
        mix = sb("mix1", [P, B, N])
        run = sb("run1", [P, B, 4, N + 1])
        xx = sb("xx1", [P, B, N])
        arg = sb("arg1", [P, B, 2, N])
        fac = sb("fac1", [P, B, 2, N])
        lns = sb("lns1", [P, B, N])
        dd = sb("dd1", [P, B, N])
        wv = sb("wv1", [P, B, N])
        rs = sb("rs1", [P, B, N])
        bv = sb("bv1", [P, B, N])
        o = sb("o1", [P, B, N])
        zeros = sb("zeros1", [P, N])
        C = [mem.enter_context(nc.psum_tensor(f"pC1_{b}", [P, N], F32)) for b in range(B)]
        V = [mem.enter_context(nc.psum_tensor(f"pV1_{b}", [P, N], F32)) for b in range(B)]
        K = [mem.enter_context(nc.psum_tensor(f"pK1_{b}", [P, N], F32)) for b in range(B)]
        R = [mem.enter_context(nc.psum_tensor(f"pR1_{b}", [P, N], F32)) for b in range(B)]

        names = ("carry_init centred squared variance logs rstd xn ln1 tsg mixed0 mixed projected maxima steps argA argB factors "
                 "sums logsum dist argC argD decays vweight gate bv numer diff blend shift gated added "
                 "centred2 squared2 variance2 log2 rstd2 centre_free carried").split()
        S = mem.enter_context(semaphores_of_phase(nc, "tm_", names))
        

        block = mem.enter_context(nc.Block())

        def at(t, b):
            return t * B + (b + 1)

        @block.sync
        def _(sp):
            sp.dma_start(vec[:, :], G.vecs).then_inc(G.att_loaded, 16)
            sp.dma_start(G.const[:, :, :], G.consts).then_inc(G.att_loaded, 16)
            sp.dma_start(X[:, :, 0:N], G.xT[:, :, 0:N]).then_inc(G.x_loaded, 16)
            sp.dma_start(G.attw[:, :, :], G.att_w).then_inc(G.att_loaded, 16)
            with sp.Fori(1, NT) as t:
                sp.wait_ge(G.x_loaded, t * 16)
                sp.dma_start(X[:, :, ds(t)], G.xT[:, :, ds(t)]).then_inc(G.x_loaded, 16)
            for dst, src in ((G.cvw[:, :, :], G.cv_w), (G.ternw[:, :, :], G.tern_w), (G.hidw[:, :, :, :], G.hid_w),
                             (G.w3w[:, :], G.w3_w)):
                sp.dma_start(dst, src).then_inc(G.ffn_loaded, 16)
            for dst, src in ((G.ssmw[:, :], G.ssm_w), (G.dtw[:, :], G.dt_w), (G.sel[:, :, :], G.selectors)):
                sp.dma_start(dst, src).then_inc(G.ssm_loaded, 16)

        @block.tensor
        def _(pe):
            pe.wait_ge(G.att_loaded, 48)
            with pe.Fori(0, NT) as t:
                pe.wait_ge(G.x_loaded, t * 16 + 16)
                for b in range(B):
                    pe.wait_ge(S["centre_free"], at(t, b))
                    nc.tensor.matmul(C[b][:], G.centre, X[:, b, ds(t)], start=True, stop=True).then_inc(S["centred"], 1)
                for b in range(B):
                    pe.wait_ge(S["squared"], at(t, b))
                    nc.tensor.matmul(V[b][:], G.ones, sq[:, b, :], start=True, stop=True).then_inc(S["variance"], 1)
                for b in range(B):
                    pe.wait_ge(S["mixed"], at(t, b))
                    for w, dst in ((0, K[b]), (1, V[b]), (2, R[b])):
                        last = nc.tensor.matmul(dst[:], G.attw[:, w, :], mix[:, b, :], start=True, stop=True)
                    last.then_inc(S["projected"], 1)
                for b in range(B):
                    pe.wait_ge(S["added"], at(t, b))
                    nc.tensor.matmul(C[b][:], G.centre, XA[:, b, ds(t)], start=True, stop=True).then_inc(S["centred2"], 1)
                for b in range(B):
                    pe.wait_ge(S["squared2"], at(t, b))
                    nc.tensor.matmul(K[b][:], G.ones, sq[:, b, :], start=True, stop=True).then_inc(S["variance2"], 1)

        @block.scalar
        def _(act):
            act.wait_ge(G.smalls_ready, 1)
            act.preload_act_table_set("natural_log_exp_and_others")
            with act.Fori(0, NT) as t:
                for b in range(B):
                    act.wait_ge(S["centred"], at(t, b))
                    nc.scalar.activation(sq[:, b, :], C[b][:], ACT.Square).then_inc(S["squared"], 1)
                for b in range(B):
                    act.wait_ge(S["variance"], at(t, b))
                    nc.scalar.activation(lnv[:, b, 0:N], V[b][:], ACT.Ln, bias=G.eps_c).then_inc(S["logs"], 1)
                    nc.scalar.activation(lnv[:, b, N:2 * N], V[b][:], ACT.Ln, bias=G.eps2_c,
                                         scale=1.0 + EPS).then_inc(S["logs"], 1)
                    act.wait_ge(S["logs"], t * (2 * B) + (2 * b + 2))
                    nc.scalar.activation(rstd[:, b, :], lnv[:, b, :], ACT.Exp, scale=-0.5).then_inc(S["rstd"], 1)
                for b in range(B):
                    act.wait_ge(S["argB"], at(t, b))
                    nc.scalar.activation(fac[:, b, :, :], arg[:, b, :, :], ACT.Exp).then_inc(S["factors"], 1)
                for b in range(B):
                    act.wait_ge(S["sums"], at(t, b))
                    nc.scalar.activation(lns[:, b, :], run[:, b, 2, 0:N], ACT.Ln).then_inc(S["logsum"], 1)
                for b in range(B):
                    act.wait_ge(S["argD"], at(t, b))
                    nc.scalar.activation(fac[:, b, :, :], arg[:, b, :, :], ACT.Exp).then_inc(S["decays"], 1)
                for b in range(B):
                    nc.scalar.activation(wv[:, b, :], dd[:, b, :], ACT.Sigmoid, scale=-1.0,
                                         bias=col("time_first")).then_inc(S["vweight"], 1)
                    nc.scalar.activation(rs[:, b, :], R[b][:], ACT.Sigmoid).then_inc(S["gate"], 1)
                act.preload_act_table_set("natural_log_exp_and_others")
                for b in range(B):
                    act.wait_ge(S["centred2"], at(t, b))
                    nc.scalar.activation(sq[:, b, :], C[b][:], ACT.Square).then_inc(S["squared2"], 1)
                for b in range(B):
                    act.wait_ge(S["variance2"], at(t, b))
                    nc.scalar.activation(lnv[:, b, 0:N], K[b][:], ACT.Ln, bias=G.eps_c).then_inc(S["log2"], 1)
                    act.wait_ge(S["log2"], at(t, b))
                    nc.scalar.activation(rstd[:, b, 0:N], lnv[:, b, 0:N], ACT.Exp, scale=-0.5).then_inc(S["rstd2"], 1)

        @block.gpsimd
        def _(pool):
            with pool.Fori(0, NT) as t:
                for b in range(B):
                    pool.wait_ge(S["shift"], at(t, b))
                    pool.wait_ge(S["gate"], at(t, b))
                    nc.gpsimd.tensor_tensor(o[:, b, :], o[:, b, :], rs[:, b, :], ALU.mult).then_inc(S["gated"], 1)
                    pool.wait_ge(S["gated"], at(t, b))
                    nc.gpsimd.tensor_tensor(XA[:, b, ds(t)], o[:, b, :], xn[:, b, :], ALU.add).then_inc(S["added"], 1)

        @block.vector
        def _(dve):
            nc.vector.memset(G.eps_c, EPS)
            nc.vector.memset(G.eps2_c, EPS * EPS)
            nc.vector.memset(zeros[:], 0.0)
            dve.wait_ge(G.att_loaded, 48)
            nc.vector.tensor_scalar(G.one_p_ts, col("time_shift"), 1.0, None, ALU.add)
            nc.vector.tensor_scalar(G.one_m_ts, col("time_shift"), -1.0, 1.0, ALU.mult, ALU.add)
            nc.vector.tensor_tensor(G.ts_m_b, col("time_shift"), col("ln1_b"), ALU.subtract).then_inc(S["carry_init"], 1)
            nc.vector.memset(G.zero_c, 0.0).then_inc(G.smalls_ready, 1)
            dve.wait_ge(S["carry_init"], 1)
            dve.wait_ge(G.smalls_ready, 1)
            for b in range(B):
                nc.vector.tensor_copy(run[:, b, 0, 0:1], G.ts_m_b)
                nc.vector.memset(run[:, b, 1, 0:1], 0.0)
                nc.vector.memset(run[:, b, 2, 0:1], 1.0).then_inc(S["centre_free"], 1)
                last = nc.vector.memset(run[:, b, 3, 0:1], 0.0)
            last.then_inc(S["carry_init"], 1)
            dve.wait_ge(S["carry_init"], 2)
            with dve.Fori(0, NT) as t:
                for b in range(B):
                    dve.wait_ge(S["rstd"], at(t, b))
                    nc.vector.tensor_tensor(xn[:, b, :], C[b][:], rstd[:, b, 0:N], ALU.mult).then_inc(S["xn"], 1)
                    nc.vector.scalar_tensor_tensor(out=run[:, b, 0, 1:N + 1], in0=C[b][:], scalar=col("ln1_w"),
                                                   in1=rstd[:, b, N:2 * N], op0=ALU.mult,
                                                   op1=ALU.mult).then_inc(S["ln1"], 1)
                for b in range(B):
                    dve.wait_ge(S["ln1"], at(t, b))
                    nc.vector.tensor_scalar(tsg[:, b, :], run[:, b, 0, 0:N], col("time_shift"), col("ln1_b"),
                                            ALU.mult, ALU.subtract).then_inc(S["tsg"], 1)
                for b in range(B):
                    dve.wait_ge(S["tsg"], at(t, b))
                    nc.vector.scalar_tensor_tensor(out=mix[:, b, :], in0=run[:, b, 0, 1:N + 1], scalar=G.one_p_ts,
                                                   in1=tsg[:, b, :], op0=ALU.mult,
                                                   op1=ALU.subtract).then_inc(S["mixed"], 1)
                for b in range(B):
                    dve.wait_ge(S["projected"], at(t, b))
                    nc.vector.tensor_tensor_scan(run[:, b, 1, 1:N + 1], K[b][:], zeros[:], run[:, b, 1, 0:1],
                                                 ALU.max, ALU.max).then_inc(S["maxima"], 1)
                for b in range(B):
                    dve.wait_ge(S["maxima"], at(t, b))
                    nc.vector.tensor_tensor(xx[:, b, :], K[b][:], run[:, b, 1, 0:N], ALU.subtract).then_inc(S["steps"], 1)
                for b in range(B):
                    dve.wait_ge(S["steps"], at(t, b))
                    nc.vector.tensor_scalar(arg[:, b, 0, :], xx[:, b, :], 0.0, -1.0, ALU.max, ALU.mult)\
                      .then_inc(S["argA"], 1)
                    nc.vector.tensor_scalar(arg[:, b, 1, :], xx[:, b, :], 0.0, None, ALU.min).then_inc(S["argB"], 1)
                for b in range(B):
                    dve.wait_ge(S["factors"], at(t, b))
                    nc.vector.tensor_tensor_scan(run[:, b, 2, 1:N + 1], fac[:, b, 0, :], fac[:, b, 1, :],
                                                 run[:, b, 2, 0:1], ALU.mult, ALU.add).then_inc(S["sums"], 1)
                for b in range(B):
                    dve.wait_ge(S["logsum"], at(t, b))
                    nc.vector.tensor_tensor(dd[:, b, :], lns[:, b, :], xx[:, b, :], ALU.subtract).then_inc(S["dist"], 1)
                for b in range(B):
                    dve.wait_ge(S["dist"], at(t, b))
                    nc.vector.tensor_scalar(arg[:, b, 0, :], dd[:, b, :], 0.0, None, ALU.min).then_inc(S["argC"], 1)
                    nc.vector.tensor_scalar(arg[:, b, 1, :], dd[:, b, :], 0.0, -1.0, ALU.max, ALU.mult)\
                      .then_inc(S["argD"], 1)
                for b in range(B):
                    dve.wait_ge(S["decays"], at(t, b))
                    nc.vector.tensor_tensor(bv[:, b, :], V[b][:], fac[:, b, 1, :], ALU.mult).then_inc(S["bv"], 1)
                for b in range(B):
                    dve.wait_ge(S["bv"], at(t, b))
                    nc.vector.tensor_tensor_scan(run[:, b, 3, 1:N + 1], fac[:, b, 0, :], bv[:, b, :],
                                                 run[:, b, 3, 0:1], ALU.mult, ALU.add).then_inc(S["numer"], 1)
                for b in range(B):
                    dve.wait_ge(S["numer"], at(t, b))
                    nc.vector.tensor_tensor(o[:, b, :], V[b][:], run[:, b, 3, 0:N], ALU.subtract).then_inc(S["diff"], 1)
                for b in range(B):
                    dve.wait_ge(S["diff"], at(t, b))
                    dve.wait_ge(S["vweight"], at(t, b))
                    nc.vector.tensor_tensor(o[:, b, :], o[:, b, :], wv[:, b, :], ALU.mult).then_inc(S["blend"], 1)
                for b in range(B):
                    dve.wait_ge(S["blend"], at(t, b))
                    nc.vector.tensor_tensor(o[:, b, :], o[:, b, :], run[:, b, 3, 0:N], ALU.add).then_inc(S["shift"], 1)
                for b in range(B):
                    dve.wait_ge(S["shift"], at(t, b))
                    nc.vector.tensor_copy(run[:, b, :, 0:1], run[:, b, :, N:N + 1]).then_inc(S["carried"], 1)
                for b in range(B):
                    dve.wait_ge(S["rstd2"], at(t, b))
                    nc.vector.scalar_tensor_tensor(out=G2[:, b, ds(t, 1)], in0=C[b][:], scalar=col("ln2_w"),
                                                   in1=rstd[:, b, 0:N], op0=ALU.mult, op1=ALU.mult)\
                      .then_inc(S["centre_free"], 1)
                dve.wait_ge(S["carried"], t * B + B)
            dve.wait_ge(S["centre_free"], NT * B + B)
            for b in range(B):
                nc.vector.tensor_copy(G2[:, b, 0:1], G2[:, b, T:T + 1])


def phase_ffn(nc, G):
    vec, X, XA, G2, col, ds = G.vec, G.X, G.XA, G.G2, G.col, G.ds
    mem = ExitStack()
    with mem:
        def sb(name, shape, dt=F32):
            return mem.enter_context(nc.sbuf_tensor(name, shape, dt))

        tsg = sb("tsg2", [P, B, N])
        mix = sb("mix2", [P, B, N])
        relu = sb("relu2", [P, 2, N])
        kk = sb("kk2", [P, B, FC, N])
        rc = sb("rc2", [P, B, N])
        z = sb("z2", [P, B, N])
        sq = sb("sq2", [P, B, N])
        lnv = sb("lnv2", [P, B, N])
        rstd = sb("rstd2", [P, B, N])
        scaled = sb("scaled2", [P, B, N])
        silu = sb("silu2", [P, 2, N])
        hA = sb("hA2", [P, B, FC, N])
        hB = kk
        w3c = sb("w3c2", [P, FC, P])
        M = [mem.enter_context(nc.psum_tensor(f"pM2_{b}", [P, N], F32)) for b in range(B)]
        Y = [mem.enter_context(nc.psum_tensor(f"pY2_{b}", [P, N], F32)) for b in range(B)]
        R = [mem.enter_context(nc.psum_tensor(f"pR2_{i}", [P, N], F32)) for i in range(4)]

        names = ("scaled_w3 centred_w3 w3_ready tsg mixed keys relus squares gate_in gate values gated residual "
                 "centredA squaredA varianceA logA rstdA scaledA addedA "
                 "centredB squaredB varianceB logB rstdB normedB "
                 "up silus hidden up1 gelu1 up2 gelu2 down "
                 "squaredC varianceC logC rstdC scaledC addedC").split()
        S = mem.enter_context(semaphores_of_phase(nc, "ffn_", names))
        block = mem.enter_context(nc.Block())

        def at(t, b):
            return t * B + (b + 1)

        def nth(t, b, f):
            return t * (B * FC) + (b * FC + f + 1)

        @block.tensor
        def _(pe):
            pe.wait_ge(G.ffn_loaded, 64)
            pe.wait_ge(S["scaled_w3"], 1)
            for f in range(FC):
                last = nc.tensor.matmul(R[0][:, f * P:(f + 1) * P], G.w3w[:, f * P:(f + 1) * P], G.centre,
                                        start=True, stop=True)
            last.then_inc(S["centred_w3"], 1)
            pe.wait_ge(S["w3_ready"], 1)
            with pe.Fori(0, NT) as t:
                for b in range(B):
                    pe.wait_ge(S["mixed"], at(t, b))
                    for f in range(FC):
                        if b:
                            pe.wait_ge(S["squares"], nth(t, b - 1, f))
                        nc.tensor.matmul(R[f][:], G.attw[:, 4 + f, :], mix[:, b, :], start=True, stop=True)\
                          .then_inc(S["keys"], 1)
                    nc.tensor.matmul(M[b][:], G.attw[:, 3, :], mix[:, b, :], start=True, stop=True)\
                      .then_inc(S["gate_in"], 1)
                for b in range(B):
                    for f in range(FC):
                        pe.wait_ge(S["squares"], nth(t, b, f))
                        last = nc.tensor.matmul(Y[b][:], G.cvw[:, f, :], kk[:, b, f, :], start=f == 0, stop=f == FC - 1)
                    last.then_inc(S["values"], 1)
                for b in range(B):
                    pe.wait_ge(S["residual"], at(t, b))
                    nc.tensor.matmul(M[b][:], G.centre, z[:, b, :], start=True, stop=True).then_inc(S["centredA"], 1)
                for b in range(B):
                    pe.wait_ge(S["squaredA"], at(t, b))
                    nc.tensor.matmul(Y[b][:], G.ones, sq[:, b, :], start=True, stop=True).then_inc(S["varianceA"], 1)
                for b in range(B):
                    pe.wait_ge(S["addedA"], at(t, b))
                    nc.tensor.matmul(M[b][:], G.centre, X[:, b, ds(t)], start=True, stop=True).then_inc(S["centredB"], 1)
                for b in range(B):
                    pe.wait_ge(S["squaredB"], at(t, b))
                    nc.tensor.matmul(Y[b][:], G.ones, sq[:, b, :], start=True, stop=True).then_inc(S["varianceB"], 1)
                for b in range(B):
                    pe.wait_ge(S["normedB"], at(t, b))
                    for f in range(FC):
                        i = b * FC + f
                        if i >= 2:
                            pe.wait_ge(S["hidden"], t * (B * FC) + (i - 1))
                        for w in range(2):
                            last = nc.tensor.matmul(R[2 * (i % 2) + w][:], G.ternw[:, w, f * P:(f + 1) * P],
                                                    z[:, b, :], start=True, stop=True)
                        last.then_inc(S["up"], 1)
                for layer, src, done, ready in ((0, hA, S["gelu1"], S["hidden"]), (1, hB, S["gelu2"], S["gelu1"])):
                    up = (S["up1"], S["up2"])[layer]
                    for b in range(B):
                        pe.wait_ge(ready, nth(t, b, FC - 1))
                        for o in range(FC):
                            i = b * FC + o
                            if i >= FC:
                                pe.wait_ge(done, t * (B * FC) + (i - FC + 1))
                            elif layer == 0:
                                pe.wait_ge(S["hidden"], nth(t, B - 1, FC - 1))
                            else:
                                pe.wait_ge(S["gelu1"], nth(t, B - 1, o))
                            for k in range(FC):
                                last = nc.tensor.matmul(R[o][:], G.hidw[:, layer, k, o * P:(o + 1) * P],
                                                        src[:, b, k, :], start=k == 0, stop=k == FC - 1)
                            last.then_inc(up, 1)
                for b in range(B):
                    pe.wait_ge(S["gelu2"], nth(t, b, FC - 1))
                    for k in range(FC):
                        last = nc.tensor.matmul(M[b][:], w3c[:, k, :], hA[:, b, k, :], start=k == 0, stop=k == FC - 1)
                    last.then_inc(S["down"], 1)
                for b in range(B):
                    pe.wait_ge(S["squaredC"], at(t, b))
                    nc.tensor.matmul(Y[b][:], G.ones, sq[:, b, :], start=True, stop=True).then_inc(S["varianceC"], 1)

        @block.scalar
        def _(act):
            def square(src, done, ready, count):
                act.wait_ge(ready, count)
                nc.scalar.activation(sq[:, b, :], src[:], ACT.Square).then_inc(done, 1)

            def inverse_root(src, variance, log, done, count):
                act.wait_ge(variance, count)
                nc.scalar.activation(lnv[:, b, :], src[:], ACT.Ln, bias=G.eps_c).then_inc(log, 1)
                act.wait_ge(log, count)
                nc.scalar.activation(rstd[:, b, :], lnv[:, b, :], ACT.Exp, scale=-0.5).then_inc(done, 1)

            with act.Fori(0, NT) as t:
                for b in range(B):
                    for f in range(FC):
                        i = b * FC + f
                        act.wait_ge(S["keys"], nth(t, b, f))
                        if i >= 2:
                            act.wait_ge(S["squares"], t * (B * FC) + (i - 1))
                        nc.scalar.activation(relu[:, i % 2, :], R[f][:], ACT.Relu).then_inc(S["relus"], 1)
                for b in range(B):
                    act.wait_ge(S["gate_in"], at(t, b))
                    nc.scalar.activation(rc[:, b, :], M[b][:], ACT.Sigmoid).then_inc(S["gate"], 1)
                act.preload_act_table_set("natural_log_exp_and_others")
                for b in range(B):
                    square(M[b], S["squaredA"], S["centredA"], at(t, b))
                for b in range(B):
                    inverse_root(Y[b], S["varianceA"], S["logA"], S["rstdA"], at(t, b))
                for b in range(B):
                    square(M[b], S["squaredB"], S["centredB"], at(t, b))
                for b in range(B):
                    inverse_root(Y[b], S["varianceB"], S["logB"], S["rstdB"], at(t, b))
                for b in range(B):
                    for f in range(FC):
                        i = b * FC + f
                        act.wait_ge(S["up"], nth(t, b, f))
                        if i >= 2:
                            act.wait_ge(S["hidden"], t * (B * FC) + (i - 1))
                        nc.scalar.activation(silu[:, i % 2, :], R[2 * (i % 2)][:], ACT.Silu,
                                             scale=col("w1_s", f)).then_inc(S["silus"], 1)
                for layer, dst, up, done in ((0, hB, S["up1"], S["gelu1"]), (1, hA, S["up2"], S["gelu2"])):
                    for b in range(B):
                        for o in range(FC):
                            act.wait_ge(up, nth(t, b, o))
                            if layer == 1 and o == 0:
                                act.wait_ge(S["up1"], nth(t, b, FC - 1))
                            nc.scalar.activation(dst[:, b, o, :], R[o][:], ACT.Gelu,
                                                 scale=col(("h1_s", "h2_s")[layer], o)).then_inc(done, 1)
                act.preload_act_table_set("natural_log_exp_and_others")
                for b in range(B):
                    square(M[b], S["squaredC"], S["down"], at(t, b))
                for b in range(B):
                    inverse_root(Y[b], S["varianceC"], S["logC"], S["rstdC"], at(t, b))

        @block.vector
        def _(dve):
            dve.wait_ge(G.ffn_loaded, 64)
            nc.vector.tensor_scalar(G.w3w[:, :], G.w3w[:, :], col("w3_s"), None, ALU.mult).then_inc(S["scaled_w3"], 1)
            dve.wait_ge(S["centred_w3"], 1)
            nc.vector.tensor_copy(w3c[:, :, :].rearrange("p a b -> p (a b)"), R[0][:]).then_inc(S["w3_ready"], 1)

            def scale(src, ready, done, count, dst):
                dve.wait_ge(ready, count)
                nc.vector.tensor_tensor(dst, src[:], rstd[:, b, :], ALU.mult).then_inc(done, 1)

            def add_residual(scaled_, added, count):
                dve.wait_ge(scaled_, count)
                nc.vector.tensor_tensor(X[:, b, ds(t)], X[:, b, ds(t)], scaled[:, b, :], ALU.add).then_inc(added, 1)

            with dve.Fori(0, NT) as t:
                for b in range(B):
                    nc.vector.tensor_scalar(tsg[:, b, :], G2[:, b, ds(t)], col("time_shift"), col("ln2_b"),
                                            ALU.mult, ALU.add).then_inc(S["tsg"], 1)
                for b in range(B):
                    dve.wait_ge(S["tsg"], at(t, b))
                    nc.vector.scalar_tensor_tensor(out=mix[:, b, :], in0=G2[:, b, ds(t, 1)], scalar=G.one_m_ts,
                                                   in1=tsg[:, b, :], op0=ALU.mult, op1=ALU.add).then_inc(S["mixed"], 1)
                for b in range(B):
                    for f in range(FC):
                        i = b * FC + f
                        dve.wait_ge(S["relus"], nth(t, b, f))
                        nc.vector.tensor_tensor(kk[:, b, f, :], R[f][:], relu[:, i % 2, :], ALU.mult)\
                          .then_inc(S["squares"], 1)
                for b in range(B):
                    dve.wait_ge(S["values"], at(t, b))
                    dve.wait_ge(S["gate"], at(t, b))
                    nc.vector.tensor_tensor(rc[:, b, :], Y[b][:], rc[:, b, :], ALU.mult).then_inc(S["gated"], 1)
                for b in range(B):
                    dve.wait_ge(S["gated"], at(t, b))
                    nc.vector.tensor_tensor(z[:, b, :], rc[:, b, :], XA[:, b, ds(t)], ALU.add).then_inc(S["residual"], 1)
                for b in range(B):
                    scale(M[b], S["rstdA"], S["scaledA"], at(t, b), scaled[:, b, :])
                for b in range(B):
                    add_residual(S["scaledA"], S["addedA"], at(t, b))
                for b in range(B):
                    scale(M[b], S["rstdB"], S["normedB"], at(t, b), z[:, b, :])
                for b in range(B):
                    for f in range(FC):
                        i = b * FC + f
                        dve.wait_ge(S["silus"], nth(t, b, f))
                        nc.vector.scalar_tensor_tensor(out=hA[:, b, f, :], in0=R[2 * (i % 2) + 1][:],
                                                       scalar=col("w2_s", f), in1=silu[:, i % 2, :],
                                                       op0=ALU.mult, op1=ALU.mult).then_inc(S["hidden"], 1)
                for b in range(B):
                    scale(M[b], S["rstdC"], S["scaledC"], at(t, b), scaled[:, b, :])
                for b in range(B):
                    add_residual(S["scaledC"], S["addedC"], at(t, b))


def phase_ssm(nc, G):
    vec, X, col, ds = G.vec, G.X, G.col, G.ds
    mem = ExitStack()
    BC = 2 * DST
    with mem:
        def sb(name, shape, dt=F32):
            return mem.enter_context(nc.sbuf_tensor(name, shape, dt))

        negA = sb("negA3", [P, CB, DST])
        wsum = sb("wsum3", [P, CB])
        sq = sb("sq3", [P, B, N])
        lnv = sb("lnv3", [P, B, N])
        rstd = sb("rstd3", [P, B, N])
        xn = sb("xn3", [P, B, N])
        raw = sb("raw3", [P, B, CB, N + TAPS - 1])
        h = sb("h3", [P, B, CB, N])
        sgate = sb("sgate3", [P, B, CB, N])
        tsb = sb("tsb3", [DTR, B, N])
        split = sb("split3", [3 * BC, B, N], BF16)
        mid = sb("mid3", [3 * BC, B, N], BF16)
        rest = sb("rest3", [3 * BC, B, N])
        dt = sb("dt3", [P, B, CB, N])
        dtu = sb("dtu3", [P, B, CB, N])
        dA = sb("dA3", [P, 2, CB, N])
        dBu = sb("dBu3", [P, 3, CB, N])
        hs = sb("hs3", [P, 2, CB, N])
        csb = sb("csb3", [P, 2, 1, N])
        prod = sb("prod3", [P, 2, CB, N])
        carry = sb("carry3", [P, B, DST, CB])
        Q = [mem.enter_context(nc.psum_tensor(f"pQ3_{i}", [P, N], F32)) for i in range(8)]

        names = ("logA wsum wmean wcentred carry0 centred squared variance logs rstd normed projected raw_in gates "
                 "conv carried h xproj ts_in split1 rest1 split2 split3 split4 dt_in magnitude expm log1p relu dt dtu "
                 "bcastB bcastC dA c_in dBu scan kept prod acc y ygated "
                 "down squaredC varianceC logC rstdC scaledC addedC").split()
        S = mem.enter_context(semaphores_of_phase(nc, "ssm_", names))
        block = mem.enter_context(nc.Block())

        def at(t, b):
            return t * B + (b + 1)

        def chunk(t, b, c):
            return t * (B * CB) + (b * CB + c + 1)

        def step(t, b, n):
            return t * (B * DST) + (b * DST + n + 1)

        @block.sync
        def _(sp):
            for dst, src in ((G.moe13[:, :, :], G.moe_w13), (G.moe2[:, :, :], G.moe_w2), (G.gatew[:, :], G.gate_w)):
                sp.dma_start(dst, src).then_inc(G.moe_loaded, 16)

        @block.tensor
        def _(pe):
            pe.wait_ge(G.ssm_loaded, 48)

            def accumulate(t, b, n):
                pe.wait_ge(S["prod"], step(t, b, n))
                for c in range(CB):
                    last = nc.tensor.matmul(Q[2 * b + c][:], G.ident, prod[:, n % 2, c, :],
                                            start=n == 0, stop=n == DST - 1)
                last.then_inc(S["acc"], 1)

            with pe.Fori(0, NT) as t:
                for b in range(B):
                    nc.tensor.matmul(Q[2 * b][:], G.centre, X[:, b, ds(t)], start=True, stop=True)\
                      .then_inc(S["centred"], 1)
                for b in range(B):
                    pe.wait_ge(S["squared"], at(t, b))
                    nc.tensor.matmul(Q[2 * b + 1][:], G.ones, sq[:, b, :], start=True, stop=True)\
                      .then_inc(S["variance"], 1)
                for b in range(B):
                    pe.wait_ge(S["normed"], at(t, b))
                    for m, q in enumerate((2 * b, 2 * b + 1, 4 + 2 * b, 5 + 2 * b)):
                        nc.tensor.matmul(Q[q][:], G.win[:, m * P:(m + 1) * P], xn[:, b, :], start=True, stop=True)\
                          .then_inc(S["projected"], 1)
                for b in range(B):
                    pe.wait_ge(S["h"], chunk(t, b, CB - 1))
                    for q, lo, hi in ((2 * b, 0, DTR), (2 * b + 1, DTR, DTR + 3 * BC)):
                        for c in range(CB):
                            last = nc.tensor.matmul(Q[q][0:hi - lo, :], G.wx[:, c, lo:hi], h[:, b, c, :],
                                                    start=c == 0, stop=c == CB - 1)
                        last.then_inc(S["xproj"], 1)
                for b in range(B):
                    pe.wait_ge(S["ts_in"], at(t, b))
                    for c in range(CB):
                        nc.tensor.matmul(Q[4 + 2 * b + c][:], G.dtw[:, c * P:(c + 1) * P], tsb[:, b, :],
                                         start=True, stop=True).then_inc(S["dt_in"], 1)
                for b in range(B):
                    for n in range(DST):
                        i = b * DST + n
                        if n == 0:
                            pe.wait_ge(S["split3"], at(t, b))
                            pe.wait_ge(S["split4"], at(t, b))
                        if i == 0:
                            pe.wait_ge(S["relu"], chunk(t, B - 1, CB - 1))
                        if i >= 2:
                            pe.wait_ge(S["dBu"], t * (B * DST) + (i - 1))
                        nc.tensor.matmul(Q[4 + i % 2][:], G.sel[:, n, :], split[:, b, :], start=True, stop=True)\
                          .then_inc(S["bcastB"], 1)
                        if i >= 2:
                            pe.wait_ge(S["c_in"], t * (B * DST) + (i - 1))
                        nc.tensor.matmul(Q[6 + i % 2][:], G.sel[:, DST + n, :], split[:, b, :],
                                         start=True, stop=True).then_inc(S["bcastC"], 1)
                        if n >= 2:
                            accumulate(t, b, n - 2)
                    accumulate(t, b, DST - 2)
                    accumulate(t, b, DST - 1)
                for b in range(B):
                    pe.wait_ge(S["ygated"], at(t, b))
                    for c in range(CB):
                        last = nc.tensor.matmul(Q[2 * b][:], G.wout[:, c, :], dt[:, b, c, :],
                                                start=c == 0, stop=c == CB - 1)
                    last.then_inc(S["down"], 1)
                for b in range(B):
                    pe.wait_ge(S["squaredC"], at(t, b))
                    nc.tensor.matmul(Q[2 * b + 1][:], G.ones, sq[:, b, :], start=True, stop=True)\
                      .then_inc(S["varianceC"], 1)
                pe.wait_ge(S["scaledC"], t * B + B)

        @block.scalar
        def _(act):
            act.preload_act_table_set("natural_log_exp_and_others")
            nc.scalar.activation(negA[:, :, :].rearrange("p c n -> p (c n)"),
                                 vec[:, VECS["A_log"]:VECS["A_log"] + CB * DST], ACT.Exp).then_inc(S["logA"], 1)

            def inverse_root(variance, log, done, count):
                act.wait_ge(variance, count)
                nc.scalar.activation(lnv[:, b, :], Q[2 * b + 1][:], ACT.Ln, bias=G.eps_c).then_inc(log, 1)
                act.wait_ge(log, count)
                nc.scalar.activation(rstd[:, b, :], lnv[:, b, :], ACT.Exp, scale=-0.5).then_inc(done, 1)

            with act.Fori(0, NT) as t:
                for b in range(B):
                    act.wait_ge(S["centred"], at(t, b))
                    nc.scalar.activation(sq[:, b, :], Q[2 * b][:], ACT.Square).then_inc(S["squared"], 1)
                for b in range(B):
                    inverse_root(S["variance"], S["logs"], S["rstd"], at(t, b))
                for b in range(B):
                    for c in range(CB):
                        act.wait_ge(S["projected"], t * (4 * B) + (4 * b + c + 1))
                        nc.scalar.activation(raw[:, b, c, TAPS - 1:TAPS - 1 + N], Q[2 * b + c][:], ACT.Copy)\
                          .then_inc(S["raw_in"], 1)
                for b in range(B):
                    act.wait_ge(S["projected"], t * (4 * B) + (4 * b + 4))
                    for c in range(CB):
                        nc.scalar.activation(sgate[:, b, c, :], Q[4 + 2 * b + c][:], ACT.Silu).then_inc(S["gates"], 1)
                for b in range(B):
                    for c in range(CB):
                        act.wait_ge(S["conv"], t * (B * CB * TAPS) + (b * CB * TAPS + (TAPS - 1) * CB + c + 1))
                        nc.scalar.activation(h[:, b, c, :], h[:, b, c, :], ACT.Silu).then_inc(S["h"], 1)
                act.preload_act_table_set("natural_log_exp_and_others")
                for b in range(B):
                    act.wait_ge(S["xproj"], t * (2 * B) + (2 * b + 1))
                    nc.scalar.activation(tsb[:, b, :], Q[2 * b][0:DTR, :], ACT.Copy).then_inc(S["ts_in"], 1)
                    act.wait_ge(S["xproj"], t * (2 * B) + (2 * b + 2))
                    nc.scalar.activation(split[:, b, :], Q[2 * b + 1][0:3 * BC, :], ACT.Copy).then_inc(S["split1"], 1)
                for b in range(B):
                    for c in range(CB):
                        z, bias = Q[4 + 2 * b + c], col("b_dt", c)
                        act.wait_ge(S["dt_in"], chunk(t, b, c))
                        nc.scalar.activation(dtu[:, b, c, :], z[:], ACT.Abs, bias=bias).then_inc(S["magnitude"], 1)
                        nc.scalar.activation(dt[:, b, c, :], z[:], ACT.Relu, bias=bias).then_inc(S["relu"], 1)
                    for c in range(CB):
                        act.wait_ge(S["magnitude"], chunk(t, b, c))
                        nc.scalar.activation(dtu[:, b, c, :], dtu[:, b, c, :], ACT.Exp, scale=-1.0).then_inc(S["expm"], 1)
                    for c in range(CB):
                        act.wait_ge(S["expm"], chunk(t, b, c))
                        nc.scalar.activation(dtu[:, b, c, :], dtu[:, b, c, :], ACT.Ln, bias=1.0).then_inc(S["log1p"], 1)
                for b in range(B):
                    act.wait_ge(S["dt"], at(t, b))
                    for n in range(DST):
                        i = b * DST + n
                        if i >= 2:
                            act.wait_ge(S["scan"], t * (B * DST) + (i - 1))
                        for c in range(CB):
                            last = nc.scalar.activation(dA[:, n % 2, c, :], dt[:, b, c, :], ACT.Exp,
                                                        scale=negA[:, c, n:n + 1])
                        last.then_inc(S["dA"], 1)
                        act.wait_ge(S["bcastC"], step(t, b, n))
                        if i >= 2:
                            act.wait_ge(S["prod"], t * (B * DST) + (i - 1))
                        nc.scalar.activation(csb[:, n % 2, 0, :], Q[6 + i % 2][:], ACT.Copy).then_inc(S["c_in"], 1)
                for b in range(B):
                    act.wait_ge(S["down"], at(t, b))
                    nc.scalar.activation(sq[:, b, :], Q[2 * b][:], ACT.Square).then_inc(S["squaredC"], 1)
                for b in range(B):
                    inverse_root(S["varianceC"], S["logC"], S["rstdC"], at(t, b))

        @block.gpsimd
        def _(pool):
            with pool.Fori(0, NT) as t:
                for b in range(B):
                    for n in range(DST):
                        i = b * DST + n
                        pool.wait_ge(S["scan"], step(t, b, n))
                        pool.wait_ge(S["c_in"], step(t, b, n))
                        if i >= 2:
                            pool.wait_ge(S["acc"], t * (B * DST) + (i - 1))
                        nc.gpsimd.tensor_tensor(prod[:, n % 2, :, :], hs[:, n % 2, :, :],
                                                csb[:, n % 2, :, :].to_broadcast([P, CB, N]), ALU.mult)\
                          .then_inc(S["prod"], 1)

        @block.vector
        def _(dve):
            dve.wait_ge(G.ssm_loaded, 48)
            nc.vector.tensor_reduce(wsum[:, :], G.wout, AX.X, ALU.add).then_inc(S["wsum"], 1)
            dve.wait_ge(S["wsum"], 1)
            nc.vector.tensor_scalar(wsum[:, :], wsum[:, :], 1.0 / P, None, ALU.mult).then_inc(S["wmean"], 1)
            dve.wait_ge(S["wmean"], 1)
            for c in range(CB):
                last = nc.vector.tensor_scalar(G.wout[:, c, :], G.wout[:, c, :], wsum[:, c:c + 1], None, ALU.subtract)
            last.then_inc(S["wcentred"], 1)
            dve.wait_ge(S["logA"], 1)
            nc.vector.tensor_scalar(negA[:, :, :], negA[:, :, :], -1.0, None, ALU.mult).then_inc(S["carry0"], 1)
            nc.vector.memset(carry[:], 0.0).then_inc(S["carry0"], 1)
            nc.vector.memset(raw[:, :, :, 0:TAPS - 1], 0.0).then_inc(S["carry0"], 1)
            dve.wait_ge(S["carry0"], 3)
            with dve.Fori(0, NT) as t:
                for b in range(B):
                    dve.wait_ge(S["rstd"], at(t, b))
                    nc.vector.tensor_tensor(xn[:, b, :], Q[2 * b][:], rstd[:, b, :], ALU.mult).then_inc(S["normed"], 1)
                for b in range(B):
                    for k in range(TAPS):
                        for c in range(CB):
                            if k == 0:
                                dve.wait_ge(S["raw_in"], chunk(t, b, c))
                                nc.vector.tensor_scalar(h[:, b, c, :], raw[:, b, c, 0:N], col("conv_w", c),
                                                        col("conv_b", c), ALU.mult, ALU.add).then_inc(S["conv"], 1)
                            else:
                                dve.wait_ge(S["conv"], t * (B * CB * TAPS) + (b * CB * TAPS + (k - 1) * CB + c + 1))
                                nc.vector.scalar_tensor_tensor(out=h[:, b, c, :], in0=raw[:, b, c, k:k + N],
                                                               scalar=col("conv_w", k * CB + c), in1=h[:, b, c, :],
                                                               op0=ALU.mult, op1=ALU.add).then_inc(S["conv"], 1)
                    dve.wait_ge(S["conv"], t * (B * CB * TAPS) + (b + 1) * CB * TAPS)
                    nc.vector.tensor_copy(raw[:, b, :, 0:TAPS - 1], raw[:, b, :, N:N + TAPS - 1]).then_inc(S["carried"], 1)
                for b in range(B):
                    dve.wait_ge(S["split1"], at(t, b))
                    nc.vector.tensor_tensor(rest[:, b, :], Q[2 * b + 1][0:3 * BC, :], split[:, b, :], ALU.subtract)\
                      .then_inc(S["rest1"], 1)
                for b in range(B):
                    dve.wait_ge(S["rest1"], at(t, b))
                    nc.vector.tensor_copy(mid[:, b, :], rest[:, b, :]).then_inc(S["split2"], 1)
                for b in range(B):
                    dve.wait_ge(S["split2"], at(t, b))
                    nc.vector.tensor_copy(split[BC:2 * BC, b, :], mid[BC:2 * BC, b, :]).then_inc(S["split3"], 1)
                    nc.vector.tensor_tensor(split[2 * BC:3 * BC, b, :], rest[2 * BC:3 * BC, b, :],
                                            mid[2 * BC:3 * BC, b, :], ALU.subtract).then_inc(S["split4"], 1)
                for b in range(B):
                    dve.wait_ge(S["log1p"], chunk(t, b, CB - 1))
                    nc.vector.tensor_tensor(dt[:, b, :, :], dt[:, b, :, :], dtu[:, b, :, :], ALU.add)\
                      .then_inc(S["dt"], 1)
                for b in range(B):
                    dve.wait_ge(S["dt"], at(t, b))
                    nc.vector.tensor_tensor(dtu[:, b, :, :], dt[:, b, :, :], h[:, b, :, :], ALU.mult)\
                      .then_inc(S["dtu"], 1)
                for b in range(B):
                    dve.wait_ge(S["dtu"], at(t, b))

                    def scan(n):
                        i = b * DST + n
                        dve.wait_ge(S["dBu"], step(t, b, n))
                        dve.wait_ge(S["dA"], step(t, b, n))
                        if i >= 2:
                            dve.wait_ge(S["prod"], t * (B * DST) + (i - 1))
                            dve.wait_ge(S["kept"], t * (B * DST) + (i - 1))
                        for c in range(CB):
                            last = nc.vector.tensor_tensor_scan(hs[:, n % 2, c, :], dA[:, n % 2, c, :],
                                                                dBu[:, n % 3, c, :], carry[:, b, n, c:c + 1],
                                                                ALU.mult, ALU.add)
                        last.then_inc(S["scan"], 1)

                    def keep(n):
                        dve.wait_ge(S["scan"], step(t, b, n))
                        nc.vector.tensor_copy(carry[:, b, n, :], hs[:, n % 2, :, N - 1]).then_inc(S["kept"], 1)

                    for n in range(DST + 1):
                        if n < DST:
                            dve.wait_ge(S["bcastB"], step(t, b, n))
                            nc.vector.tensor_tensor(dBu[:, n % 3, :, :], dtu[:, b, :, :],
                                                    Q[4 + n % 2][:].unsqueeze(1).to_broadcast([P, CB, N]), ALU.mult)\
                              .then_inc(S["dBu"], 1)
                        if n >= 1:
                            scan(n - 1)
                        if n >= 2:
                            keep(n - 2)
                    keep(DST - 1)
                    dve.wait_ge(S["kept"], step(t, b, DST - 1))
                    dve.wait_ge(S["acc"], step(t, b, DST - 1))
                    for c in range(CB):
                        nc.vector.scalar_tensor_tensor(out=h[:, b, c, :], in0=h[:, b, c, :], scalar=col("D", c),
                                                       in1=Q[2 * b + c][:], op0=ALU.mult, op1=ALU.add)\
                          .then_inc(S["y"], 1)
                    dve.wait_ge(S["y"], chunk(t, b, CB - 1))
                    nc.vector.tensor_tensor(dt[:, b, :, :], h[:, b, :, :], sgate[:, b, :, :], ALU.mult)\
                      .then_inc(S["ygated"], 1)
                for b in range(B):
                    dve.wait_ge(S["rstdC"], at(t, b))
                    nc.vector.tensor_tensor(xn[:, b, :], Q[2 * b][:], rstd[:, b, :], ALU.mult).then_inc(S["scaledC"], 1)
                for b in range(B):
                    dve.wait_ge(S["scaledC"], at(t, b))
                    nc.vector.tensor_tensor(X[:, b, ds(t)], X[:, b, ds(t)], xn[:, b, :], ALU.add).then_inc(S["addedC"], 1)
                dve.wait_ge(S["addedC"], t * B + B)


def phase_moe(nc, G):
    vec, X, col, ds = G.vec, G.X, G.col, G.ds
    mem = ExitStack()
    TC = N // P
    U = E * FC
    with mem:
        def sb(name, shape, dt=F32):
            return mem.enter_context(nc.sbuf_tensor(name, shape, dt))

        wmean = sb("wmean4", [P, U])
        iota = sb("iota4", [P, E])
        sq = sb("sq4", [P, B, N])
        lnv = sb("lnv4", [P, B, N])
        rstd = sb("rstd4", [P, B, N])
        xn = sb("xn4", [P, B, N])
        turn = sb("turn4", [P, 1])
        logits = sb("logits4", [P, B, TC, E])
        best = sb("best4", [P, B, TC, E])
        where = sb("where4", [P, B, TC, E], mybir.dt.uint32)
        wheref = sb("wheref4", [P, B, TC, 2])
        gap = sb("gap4", [P, B, TC])
        den = sb("den4", [P, B, TC])
        share = sb("share4", [P, B, TC, 2])
        pick = sb("pick4", [P, B, 2, TC, E])
        comb = sb("comb4", [P, B, TC, E])
        xs = sb("xs4", [P, 2, N])
        silu = sb("silu4", [P, 2, N])
        hid = sb("hid4", [P, 3, N])
        M = [mem.enter_context(nc.psum_tensor(f"pM4_{b}", [P, N], F32)) for b in range(B)]
        Y = [mem.enter_context(nc.psum_tensor(f"pY4_{b}", [P, N], F32)) for b in range(B)]
        R = [mem.enter_context(nc.psum_tensor(f"pR4_{i}", [P, N], F32)) for i in range(4)]

        names = ("iota wsum wmean wcentred centred squared variance logs rstd normed scores logits best where wheref "
                 "gap share2 den share1 share1b picks comb spread scaled_x up silus hidden down "
                 "squaredC varianceC logC rstdC scaledC addedC stored").split()
        S = mem.enter_context(semaphores_of_phase(nc, "moe_", names))
        block = mem.enter_context(nc.Block())

        def at(t, b):
            return t * B + (b + 1)

        def unit(t, b, i):
            return t * (B * U) + (b * U + i + 1)

        def expert(t, b, e):
            return t * (B * E) + (b * E + e + 1)

        @block.sync
        def _(sp):
            sp.dma_start(iota[:, :], G.iota_c).then_inc(S["iota"], 16)
            with sp.Fori(0, NT) as t:
                for b in range(B):
                    sp.wait_ge(S["addedC"], at(t, b))
                    sp.dma_start(G.outT[:, b, ds(t)], X[:, b, ds(t)]).then_inc(S["stored"], 16)
            sp.wait_ge(S["stored"], NT * B * 16)

        @block.tensor
        def _(pe):
            pe.wait_ge(G.moe_loaded, 48)
            pe.wait_ge(S["wcentred"], 1)

            def spread(t, b, e):
                if e >= 2:
                    pe.wait_ge(S["scaled_x"], expert(t, b, e - 2))
                for j in range(TC):
                    last = nc.tensor.matmul(M[e % 2][:, j * P:(j + 1) * P],
                                            comb[:, b, j, e:e + 1].to_broadcast([P, P]), G.ident,
                                            start=True, stop=True)
                last.then_inc(S["spread"], 1)

            def down(t, b, i):
                pe.wait_ge(S["hidden"], unit(t, b, i))
                nc.tensor.matmul(Y[b][:], G.moe2[:, i, :], hid[:, i % 3, :], start=i == 0, stop=i == U - 1)\
                  .then_inc(S["down"], 1)

            with pe.Fori(0, NT) as t:
                for b in range(B):
                    nc.tensor.matmul(M[b][:], G.centre, X[:, b, ds(t)], start=True, stop=True).then_inc(S["centred"], 1)
                for b in range(B):
                    pe.wait_ge(S["squared"], at(t, b))
                    nc.tensor.matmul(Y[b][:], G.ones, sq[:, b, :], start=True, stop=True).then_inc(S["variance"], 1)
                for b in range(B):
                    pe.wait_ge(S["normed"], at(t, b))
                    for j in range(TC):
                        last = nc.tensor.matmul(M[b][:, j * E:(j + 1) * E], xn[:, b, j * P:(j + 1) * P], G.gatew[:, :],
                                                start=True, stop=True)
                    last.then_inc(S["scores"], 1)
                for b in range(B):
                    pe.wait_ge(S["comb"], t * B + B)
                    spread(t, b, 0)
                    for i in range(U):
                        e, f = divmod(i, FC)
                        if f == 1 and e + 1 < E:
                            spread(t, b, e + 1)
                        if b * U + i >= 2:
                            pe.wait_ge(S["hidden"], t * (B * U) + (b * U + i - 1))
                        nc.tensor.matmul(R[2 * (i % 2)][:], G.moe13[:, e, f * P:(f + 1) * P], xn[:, b, :],
                                         start=True, stop=True)
                        pe.wait_ge(S["scaled_x"], expert(t, b, e))
                        nc.tensor.matmul(R[2 * (i % 2) + 1][:], G.moe13[:, e, FFN + f * P:FFN + (f + 1) * P],
                                         xs[:, e % 2, :], start=True, stop=True).then_inc(S["up"], 1)
                        if i >= 2:
                            down(t, b, i - 2)
                    down(t, b, U - 2)
                    down(t, b, U - 1)
                for b in range(B):
                    pe.wait_ge(S["squaredC"], at(t, b))
                    nc.tensor.matmul(M[b][:], G.ones, sq[:, b, :], start=True, stop=True).then_inc(S["varianceC"], 1)
                pe.wait_ge(S["scaledC"], t * B + B)

        @block.scalar
        def _(act):
            def inverse_root(src, variance, log, done, count):
                act.wait_ge(variance, count)
                nc.scalar.activation(lnv[:, b, :], src[:], ACT.Ln, bias=G.eps_c).then_inc(log, 1)
                act.wait_ge(log, count)
                nc.scalar.activation(rstd[:, b, :], lnv[:, b, :], ACT.Exp, scale=-0.5).then_inc(done, 1)

            with act.Fori(0, NT) as t:
                act.preload_act_table_set("natural_log_exp_and_others")
                for b in range(B):
                    act.wait_ge(S["centred"], at(t, b))
                    nc.scalar.activation(sq[:, b, :], M[b][:], ACT.Square).then_inc(S["squared"], 1)
                for b in range(B):
                    inverse_root(Y[b], S["variance"], S["logs"], S["rstd"], at(t, b))
                for b in range(B):
                    act.wait_ge(S["gap"], at(t, b))
                    nc.scalar.activation(share[:, b, :, 1], gap[:, b, :], ACT.Exp).then_inc(S["share2"], 1)
                for b in range(B):
                    for i in range(U):
                        act.wait_ge(S["up"], unit(t, b, i))
                        if b * U + i >= 2:
                            act.wait_ge(S["hidden"], t * (B * U) + (b * U + i - 1))
                        nc.scalar.activation(silu[:, i % 2, :], R[2 * (i % 2)][:], ACT.Silu).then_inc(S["silus"], 1)
                act.preload_act_table_set("natural_log_exp_and_others")
                for b in range(B):
                    act.wait_ge(S["down"], unit(t, b, U - 1))
                    nc.scalar.activation(sq[:, b, :], Y[b][:], ACT.Square).then_inc(S["squaredC"], 1)
                for b in range(B):
                    inverse_root(M[b], S["varianceC"], S["logC"], S["rstdC"], at(t, b))

        @block.vector
        def _(dve):
            dve.wait_ge(G.moe_loaded, 48)
            dve.wait_ge(S["iota"], 16)
            nc.vector.tensor_reduce(wmean[:, :], G.moe2[:, :, :], AX.X, ALU.add).then_inc(S["wsum"], 1)
            dve.wait_ge(S["wsum"], 1)
            nc.vector.tensor_scalar(wmean[:, :], wmean[:, :], 1.0 / P, None, ALU.mult).then_inc(S["wmean"], 1)
            dve.wait_ge(S["wmean"], 1)
            nc.vector.tensor_tensor(G.moe2[:, :, :], G.moe2[:, :, :], wmean[:, :].unsqueeze(2).to_broadcast([P, U, P]),
                                    ALU.subtract).then_inc(S["wcentred"], 1)
            gate_b = vec[:, VECS["gate_b"]:VECS["gate_b"] + E].unsqueeze(1).to_broadcast([P, TC, E])
            with dve.Fori(0, NT) as t:
                for b in range(B):
                    dve.wait_ge(S["rstd"], at(t, b))
                    nc.vector.tensor_tensor(xn[:, b, :], M[b][:], rstd[:, b, :], ALU.mult).then_inc(S["normed"], 1)
                for b in range(B):
                    dve.wait_ge(S["scores"], at(t, b))
                    nc.vector.tensor_tensor(logits[:, b, :, :],
                                            M[b][:, 0:TC * E].rearrange("p (j e) -> p j e", j=TC), gate_b, ALU.add)\
                      .then_inc(S["logits"], 1)
                dve.wait_ge(S["logits"], t * B + B)
                nc.vector.memset(turn[:, :], 0.0)
                for b in range(B):
                    for j in range(TC):
                        last = nc.vector.max(best[:, b, j, :], logits[:, b, j, :])
                    last.then_inc(S["best"], 1)
                for b in range(B):
                    dve.wait_ge(S["best"], at(t, b))
                    nc.vector.tensor_tensor(gap[:, b, :], best[:, b, :, 1], best[:, b, :, 0], ALU.subtract)\
                      .then_inc(S["gap"], 1)
                    for j in range(TC):
                        last = nc.vector.max_index(where[:, b, j, :], best[:, b, j, :], logits[:, b, j, :])
                    last.then_inc(S["where"], 1)
                for b in range(B):
                    dve.wait_ge(S["where"], at(t, b))
                    nc.vector.tensor_copy(wheref[:, b, :, :], where[:, b, :, 0:2]).then_inc(S["wheref"], 1)
                for b in range(B):
                    dve.wait_ge(S["share2"], at(t, b))
                    nc.vector.tensor_scalar(den[:, b, :], share[:, b, :, 1], 1.0, None, ALU.add).then_inc(S["den"], 1)
                for b in range(B):
                    dve.wait_ge(S["den"], at(t, b))
                    nc.vector.reciprocal(share[:, b, :, 0], den[:, b, :]).then_inc(S["share1"], 1)
                for b in range(B):
                    dve.wait_ge(S["share1"], at(t, b))
                    nc.vector.tensor_tensor(share[:, b, :, 1], share[:, b, :, 1], share[:, b, :, 0], ALU.mult)\
                      .then_inc(S["share1b"], 1)
                for b in range(B):
                    dve.wait_ge(S["share1b"], at(t, b))
                    dve.wait_ge(S["wheref"], at(t, b))
                    for r in range(2):
                        for j in range(TC):
                            last = nc.vector.tensor_scalar(pick[:, b, r, j, :], iota[:, :], wheref[:, b, j, r:r + 1],
                                                           share[:, b, j, r:r + 1], ALU.is_equal, ALU.mult)
                    last.then_inc(S["picks"], 1)
                for b in range(B):
                    dve.wait_ge(S["picks"], at(t, b))
                    nc.vector.tensor_tensor(comb[:, b, :, :], pick[:, b, 0, :, :], pick[:, b, 1, :, :], ALU.add)\
                      .then_inc(S["comb"], 1)
                for b in range(B):
                    def scale_x(e):
                        dve.wait_ge(S["spread"], expert(t, b, e))
                        if b * E + e >= 2:
                            dve.wait_ge(S["up"], t * (B * U) + (b * E + e - 1) * FC)
                        nc.vector.tensor_tensor(xs[:, e % 2, :], xn[:, b, :], M[e % 2][:], ALU.mult)\
                          .then_inc(S["scaled_x"], 1)

                    scale_x(0)
                    for i in range(U):
                        e, f = divmod(i, FC)
                        if f == 2 and e + 1 < E:
                            scale_x(e + 1)
                        dve.wait_ge(S["silus"], unit(t, b, i))
                        if b * U + i >= 3:
                            dve.wait_ge(S["down"], t * (B * U) + (b * U + i - 2))
                        nc.vector.tensor_tensor(hid[:, i % 3, :], R[2 * (i % 2) + 1][:], silu[:, i % 2, :], ALU.mult)\
                          .then_inc(S["hidden"], 1)
                for b in range(B):
                    dve.wait_ge(S["rstdC"], at(t, b))
                    nc.vector.tensor_tensor(xn[:, b, :], Y[b][:], rstd[:, b, :], ALU.mult).then_inc(S["scaledC"], 1)
                for b in range(B):
                    dve.wait_ge(S["scaledC"], at(t, b))
                    nc.vector.tensor_tensor(X[:, b, ds(t)], X[:, b, ds(t)], xn[:, b, :], ALU.add).then_inc(S["addedC"], 1)
                dve.wait_ge(S["addedC"], t * B + B)


def kernel(**inputs):
    import numpy as np
    import concourse.bacc as bacc
    from concourse.bass_utils import run_bass_kernel_spmd

    a = {k: np.asarray(v) for k, v in inputs.items()}

    def chunks(v):
        return v.reshape(-1, P).T

    def rows(w):
        return w.reshape(-1, P, w.shape[-1]).transpose(1, 0, 2)

    L0, L1, F0, F1 = "L0_attn_", "L1_attn_", "L0_ffn_", "L1_ffn_"
    vecs = np.concatenate([
        a[L0 + "time_first"][:, None], a[L0 + "time_shift"].reshape(P, 1), a[L0 + "ln1_w"][:, None],
        a[L0 + "ln1_b"][:, None], a[L0 + "ln2_w"][:, None], a[L0 + "ln2_b"][:, None],
        chunks(a[F0 + "w1_s"]), chunks(a[F0 + "w2_s"]), chunks(a[F0 + "h1_s"]), chunks(a[F0 + "h2_s"]),
        chunks(a[F0 + "w3_s"]),
        a[L1 + "conv_w"].reshape(TAPS, CB, P).transpose(2, 0, 1).reshape(P, TAPS * CB),
        chunks(a[L1 + "conv_b"]), chunks(a[L1 + "b_dt"]), chunks(a[L1 + "D"]),
        rows(a[L1 + "A_log"]).reshape(P, CB * DST), np.broadcast_to(a[F1 + "gate_b"], (P, E)),
    ], axis=1)
    wxs = a[L1 + "W_x"]
    wxs = np.concatenate([wxs[:, 0:DTR]] + [wxs[:, DTR:]] * 3, axis=1)
    selectors = np.zeros((3 * 2 * DST, 2 * DST, P), np.float32)
    for n in range(2 * DST):
        selectors[n::2 * DST, n, :] = 1.0
    bf16 = np.dtype("bfloat16")
    arrays = {
        "xT": a[L0 + "x"].transpose(2, 0, 1),
        "vecs": vecs,
        "att_w": np.concatenate([a[L0 + w].T for w in ("Wk", "Wv", "Wr", "Wcr", "Wck")], axis=1).reshape(P, 8, P),
        "cv_w": rows(a[L0 + "Wcv"].T),
        "tern_w": np.stack([a[F0 + "w1_w"].T, a[F0 + "w2_w"].T], axis=1),
        "hid_w": np.stack([rows(a[F0 + "h1_w"].T), rows(a[F0 + "h2_w"].T)], axis=1),
        "w3_w": a[F0 + "w3_w"],
        "ssm_w": np.concatenate([a[L1 + "W_in"], rows(wxs).reshape(P, -1), rows(a[L1 + "W_out"]).reshape(P, -1)],
                                axis=1),
        "dt_w": a[L1 + "W_dt"],
        "moe_w13": np.concatenate([a[F1 + "w1"], a[F1 + "w3"]], axis=2).transpose(1, 0, 2),
        "moe_w2": rows(a[F1 + "w2"].reshape(E * FFN, P)),
        "gate_w": a[F1 + "gate_w"],
        "consts": np.stack([np.eye(P), np.eye(P) - 1.0 / P, np.full((P, P), 1.0 / P)], axis=1).astype(np.float32),
        "selectors": selectors.astype(bf16),
        "iota_c": np.broadcast_to(np.arange(E, dtype=np.float32), (P, E)),
    }
    nc = bacc.Bacc("TRN2", target_bir_lowering=False, num_devices=1)
    args = {}
    for name, value in arrays.items():
        arrays[name] = value = np.ascontiguousarray(value)
        args[name] = nc.dram_tensor(name, value.shape, mybir.dt.from_np(value.dtype), kind="ExternalInput").ap()
    outT = nc.dram_tensor("outT", (P, B, T), F32, kind="ExternalOutput").ap()
    build(nc, outT=outT, **args)
    r = run_bass_kernel_spmd(nc, [arrays], core_ids=[0])
    return np.ascontiguousarray(r.results[0]["outT"].transpose(1, 2, 0))
```

```python
from contextlib import ExitStack, contextmanager

import concourse.bass as bass
from concourse import mybir

F32 = mybir.dt.float32
BF16 = mybir.dt.bfloat16
F16 = mybir.dt.float16
ALU = mybir.AluOpType
ACT = mybir.ActivationFunctionType
AX = mybir.AxisListType

P = 128
B = 2
T = 2048
N = 512
NT = T // N
FFN = 512
FC = FFN // P
INTER = 256
CB = INTER // P
DST = 16
DTR = 64
TAPS = 4
E = 8
EPS = 1e-5
WS = 64.0

VECS = {}
NV = 0
for _name, _count in (
    ("time_first", 1), ("time_shift", 1), ("ln1_w", 1), ("ln1_b", 1), ("ln2_w", 1), ("ln2_b", 1),
    ("w1_s", FC), ("w2_s", FC), ("h1_s", FC), ("h2_s", FC), ("w3_s", 1),
    ("conv_w", TAPS * CB), ("conv_b", CB), ("b_dt", CB), ("D", CB), ("A_log", CB * DST), ("gate_b", E),
):
    VECS[_name] = NV
    NV += _count


def build(nc, xT, vecs, att_w, cv_w, tern_w, hid_w, w3_w, ssm_w, dt_w, moe_w13, moe_w2, gate_w, consts, selectors, iota_c, outT,
          last_phase=4):
    ctx = ExitStack()
    with ctx:
        def sb(name, shape, dt=F32, scope=ctx):
            return scope.enter_context(nc.sbuf_tensor(name, shape, dt))

        def sem(name):
            return ctx.enter_context(nc.semaphore(name))

        X = sb("X", [P, B, T])
        vec = sb("vec", [P, NV])
        const = sb("const", [P, 3, P])
        ident, centre, ones = const[:, 0, :], const[:, 1, :], const[:, 2, :]
        sel = sb("sel", [3 * 2 * DST, 2 * DST, P], BF16)
        ssmw = sb("ssmw", [P, 2 * INTER + CB * (DTR + 6 * DST) + CB * P])
        win = ssmw[:, 0:2 * INTER]
        wx = ssmw[:, 2 * INTER:2 * INTER + CB * (DTR + 6 * DST)].rearrange("p (c m) -> p c m", c=CB)
        wout = ssmw[:, 2 * INTER + CB * (DTR + 6 * DST):].rearrange("p (c m) -> p c m", c=CB)
        dtw = sb("dtw", [DTR, INTER])
        gatew = sb("gatew", [P, E])
        small = sb("small", [P, 8])
        eps_c, eps2_c, one_p_ts, one_m_ts, ts_m_b, zero_c = (small[:, i:i + 1] for i in range(6))

        def col(name, i=0):
            return vec[:, VECS[name] + i:VECS[name] + i + 1]

        att_loaded, ffn_loaded, ssm_loaded, moe_loaded = (
            sem(n) for n in ("att_loaded", "ffn_loaded", "ssm_loaded", "moe_loaded"))
        x_loaded = sem("x_loaded")
        smalls_ready = sem("smalls_ready")

        def ds(t, extra=0, size=N):
            return bass.ds(t * N + extra, size)

        with ExitStack() as mem12:
            XA = sb("XA", [P, B, T], scope=mem12)
            G2 = sb("G2", [P, B, T + 1], scope=mem12)
            attw = sb("attw", [P, 8, P], scope=mem12)
            cvw = sb("cvw", [P, FC, P], scope=mem12)
            ternw = sb("ternw", [P, 2, FFN], scope=mem12)
            hidw = sb("hidw", [P, 2, FC, FFN], scope=mem12)
            w3w = sb("w3w", [P, FFN], scope=mem12)
            G = Shared()
            G.X, G.XA, G.G2, G.vec, G.const, G.ident, G.centre = (
                X, XA, G2, vec, const, ident, centre)
            G.ones, G.sel, G.attw, G.cvw, G.ternw, G.hidw, G.w3w = (
                ones, sel, attw, cvw, ternw, hidw, w3w)
            G.ssmw, G.win, G.wx, G.wout, G.dtw, G.gatew, G.eps_c = (
                ssmw, win, wx, wout, dtw, gatew, eps_c)
            G.eps2_c, G.one_p_ts, G.one_m_ts, G.ts_m_b, G.zero_c, G.col, G.ds = (
                eps2_c, one_p_ts, one_m_ts, ts_m_b, zero_c, col, ds)
            G.x_loaded, G.att_loaded, G.ffn_loaded, G.ssm_loaded, G.moe_loaded, G.smalls_ready, G.xT = (
                x_loaded, att_loaded, ffn_loaded, ssm_loaded, moe_loaded, smalls_ready, xT)
            G.vecs, G.att_w, G.cv_w, G.tern_w, G.hid_w, G.w3_w, G.ssm_w = (
                vecs, att_w, cv_w, tern_w, hid_w, w3_w, ssm_w)
            G.dt_w, G.moe_w13, G.moe_w2, G.gate_w, G.consts, G.selectors, G.iota_c = (
                dt_w, moe_w13, moe_w2, gate_w, consts, selectors, iota_c)
            G.outT = (
                outT)
            phase_time_mix(nc, G)
            if last_phase == 1:
                return finish(nc, ctx, XA, outT)
            phase_ffn(nc, G)
        moe13 = sb("moe13", [P, E, 2 * FFN])
        moe2 = sb("moe2", [P, E * FC, P])
        G.moe13, G.moe2 = moe13, moe2
        if last_phase >= 3:
            phase_ssm(nc, G)
        if last_phase >= 4:
            phase_moe(nc, G)
        else:
            finish(nc, ctx, X, outT)


def finish(nc, ctx, src, outT):
    done = ctx.enter_context(nc.semaphore("out_done"))
    with nc.Block() as block:
        @block.sync
        def _(sp):
            sp.dma_start(outT, src[:, :, :]).then_inc(done, 16)
            sp.wait_ge(done, 16)


class Shared:
    pass


@contextmanager
def semaphores_of_phase(nc, prefix, names):
    sems = {n: nc.alloc_semaphore(name=prefix + n) for n in names}
    yield sems
    nc.clear_and_free_semaphores(list(sems.values()))
    nc.all_engine_barrier()


def phase_time_mix(nc, G):
    vec, X, XA, G2, col, ds = G.vec, G.X, G.XA, G.G2, G.col, G.ds
    mem = ExitStack()
    with mem:
        def sb(name, shape, dt=F32):
            return mem.enter_context(nc.sbuf_tensor(name, shape, dt))

        sq = sb("sq1", [P, B, N])
        lnv = sb("lnv1", [P, B, 2 * N])
        rstd = sb("rstd1", [P, B, 2 * N])
        xn = sb("xn1", [P, B, N])
        tsg = sb("tsg1", [P, B, N])
        mix = sb("mix1", [P, B, N])
        run = sb("run1", [P, B, 4, N + 1])
        xx = sb("xx1", [P, B, N])
        arg = sb("arg1", [P, B, 2, N])
        fac = sb("fac1", [P, B, 2, N])
        lns = sb("lns1", [P, B, N])
        dd = sb("dd1", [P, B, N])
        wv = sb("wv1", [P, B, N])
        rs = sb("rs1", [P, B, N])
        bv = sb("bv1", [P, B, N])
        o = sb("o1", [P, B, N])
        zeros = sb("zeros1", [P, N])
        C = [mem.enter_context(nc.psum_tensor(f"pC1_{b}", [P, N], F32)) for b in range(B)]
        V = [mem.enter_context(nc.psum_tensor(f"pV1_{b}", [P, N], F32)) for b in range(B)]
        K = [mem.enter_context(nc.psum_tensor(f"pK1_{b}", [P, N], F32)) for b in range(B)]
        R = [mem.enter_context(nc.psum_tensor(f"pR1_{b}", [P, N], F32)) for b in range(B)]

        names = ("carry_init centred squared variance logs rstd xn ln1 tsg mixed0 mixed projected maxima steps argA argB factors "
                 "sums logsum dist argC argD decays vweight gate bv numer diff blend shift gated added "
                 "centred2 squared2 variance2 log2 rstd2 centre_free carried").split()
        S = mem.enter_context(semaphores_of_phase(nc, "tm_", names))
        

        block = mem.enter_context(nc.Block())

        def at(t, b):
            return t * B + (b + 1)

        @block.sync
        def _(sp):
            sp.dma_start(vec[:, :], G.vecs).then_inc(G.att_loaded, 16)
            sp.dma_start(G.const[:, :, :], G.consts).then_inc(G.att_loaded, 16)
            sp.dma_start(X[:, :, 0:N], G.xT[:, :, 0:N]).then_inc(G.x_loaded, 16)
            sp.dma_start(G.attw[:, :, :], G.att_w).then_inc(G.att_loaded, 16)
            with sp.Fori(1, NT) as t:
                sp.wait_ge(G.x_loaded, t * 16)
                sp.dma_start(X[:, :, ds(t)], G.xT[:, :, ds(t)]).then_inc(G.x_loaded, 16)
            for dst, src in ((G.cvw[:, :, :], G.cv_w), (G.ternw[:, :, :], G.tern_w), (G.hidw[:, :, :, :], G.hid_w),
                             (G.w3w[:, :], G.w3_w)):
                sp.dma_start(dst, src).then_inc(G.ffn_loaded, 16)
            for dst, src in ((G.ssmw[:, :], G.ssm_w), (G.dtw[:, :], G.dt_w), (G.sel[:, :, :], G.selectors)):
                sp.dma_start(dst, src).then_inc(G.ssm_loaded, 16)

        @block.tensor
        def _(pe):
            pe.wait_ge(G.att_loaded, 48)
            with pe.Fori(0, NT) as t:
                pe.wait_ge(G.x_loaded, t * 16 + 16)
                for b in range(B):
                    pe.wait_ge(S["centre_free"], at(t, b))
                    nc.tensor.matmul(C[b][:], G.centre, X[:, b, ds(t)], start=True, stop=True).then_inc(S["centred"], 1)
                for b in range(B):
                    pe.wait_ge(S["squared"], at(t, b))
                    nc.tensor.matmul(V[b][:], G.ones, sq[:, b, :], start=True, stop=True).then_inc(S["variance"], 1)
                for b in range(B):
                    pe.wait_ge(S["mixed"], at(t, b))
                    for w, dst in ((0, K[b]), (1, V[b]), (2, R[b])):
                        last = nc.tensor.matmul(dst[:], G.attw[:, w, :], mix[:, b, :], start=True, stop=True)
                    last.then_inc(S["projected"], 1)
                for b in range(B):
                    pe.wait_ge(S["added"], at(t, b))
                    nc.tensor.matmul(C[b][:], G.centre, XA[:, b, ds(t)], start=True, stop=True).then_inc(S["centred2"], 1)
                for b in range(B):
                    pe.wait_ge(S["squared2"], at(t, b))
                    nc.tensor.matmul(K[b][:], G.ones, sq[:, b, :], start=True, stop=True).then_inc(S["variance2"], 1)

        @block.scalar
        def _(act):
            act.wait_ge(G.smalls_ready, 1)
            act.preload_act_table_set("natural_log_exp_and_others")
            with act.Fori(0, NT) as t:
                for b in range(B):
                    act.wait_ge(S["centred"], at(t, b))
                    nc.scalar.activation(sq[:, b, :], C[b][:], ACT.Square).then_inc(S["squared"], 1)
                for b in range(B):
                    act.wait_ge(S["variance"], at(t, b))
                    nc.scalar.activation(lnv[:, b, 0:N], V[b][:], ACT.Ln, bias=G.eps_c).then_inc(S["logs"], 1)
                    nc.scalar.activation(lnv[:, b, N:2 * N], V[b][:], ACT.Ln, bias=G.eps2_c,
                                         scale=1.0 + EPS).then_inc(S["logs"], 1)
                    act.wait_ge(S["logs"], t * (2 * B) + (2 * b + 2))
                    nc.scalar.activation(rstd[:, b, :], lnv[:, b, :], ACT.Exp, scale=-0.5).then_inc(S["rstd"], 1)
                for b in range(B):
                    act.wait_ge(S["argB"], at(t, b))
                    nc.scalar.activation(fac[:, b, :, :], arg[:, b, :, :], ACT.Exp).then_inc(S["factors"], 1)
                for b in range(B):
                    act.wait_ge(S["sums"], at(t, b))
                    nc.scalar.activation(lns[:, b, :], run[:, b, 2, 0:N], ACT.Ln).then_inc(S["logsum"], 1)
                for b in range(B):
                    act.wait_ge(S["argD"], at(t, b))
                    nc.scalar.activation(fac[:, b, :, :], arg[:, b, :, :], ACT.Exp).then_inc(S["decays"], 1)
                for b in range(B):
                    nc.scalar.activation(wv[:, b, :], dd[:, b, :], ACT.Sigmoid, scale=-1.0,
                                         bias=col("time_first")).then_inc(S["vweight"], 1)
                    nc.scalar.activation(rs[:, b, :], R[b][:], ACT.Sigmoid).then_inc(S["gate"], 1)
                act.preload_act_table_set("natural_log_exp_and_others")
                for b in range(B):
                    act.wait_ge(S["centred2"], at(t, b))
                    nc.scalar.activation(sq[:, b, :], C[b][:], ACT.Square).then_inc(S["squared2"], 1)
                for b in range(B):
                    act.wait_ge(S["variance2"], at(t, b))
                    nc.scalar.activation(lnv[:, b, 0:N], K[b][:], ACT.Ln, bias=G.eps_c).then_inc(S["log2"], 1)
                    act.wait_ge(S["log2"], at(t, b))
                    nc.scalar.activation(rstd[:, b, 0:N], lnv[:, b, 0:N], ACT.Exp, scale=-0.5).then_inc(S["rstd2"], 1)

        @block.gpsimd
        def _(pool):
            with pool.Fori(0, NT) as t:
                for b in range(B):
                    pool.wait_ge(S["shift"], at(t, b))
                    pool.wait_ge(S["gate"], at(t, b))
                    nc.gpsimd.tensor_tensor(o[:, b, :], o[:, b, :], rs[:, b, :], ALU.mult).then_inc(S["gated"], 1)
                    pool.wait_ge(S["gated"], at(t, b))
                    nc.gpsimd.tensor_tensor(XA[:, b, ds(t)], o[:, b, :], xn[:, b, :], ALU.add).then_inc(S["added"], 1)

        @block.vector
        def _(dve):
            nc.vector.memset(G.eps_c, EPS)
            nc.vector.memset(G.eps2_c, EPS * EPS)
            nc.vector.memset(zeros[:], 0.0)
            dve.wait_ge(G.att_loaded, 48)
            nc.vector.tensor_scalar(G.one_p_ts, col("time_shift"), 1.0, None, ALU.add)
            nc.vector.tensor_scalar(G.one_m_ts, col("time_shift"), -1.0, 1.0, ALU.mult, ALU.add)
            nc.vector.tensor_tensor(G.ts_m_b, col("time_shift"), col("ln1_b"), ALU.subtract).then_inc(S["carry_init"], 1)
            nc.vector.memset(G.zero_c, 0.0).then_inc(G.smalls_ready, 1)
            dve.wait_ge(S["carry_init"], 1)
            dve.wait_ge(G.smalls_ready, 1)
            for b in range(B):
                nc.vector.tensor_copy(run[:, b, 0, 0:1], G.ts_m_b)
                nc.vector.memset(run[:, b, 1, 0:1], 0.0)
                nc.vector.memset(run[:, b, 2, 0:1], 1.0).then_inc(S["centre_free"], 1)
                last = nc.vector.memset(run[:, b, 3, 0:1], 0.0)
            last.then_inc(S["carry_init"], 1)
            dve.wait_ge(S["carry_init"], 2)
            with dve.Fori(0, NT) as t:
                for b in range(B):
                    dve.wait_ge(S["rstd"], at(t, b))
                    nc.vector.tensor_tensor(xn[:, b, :], C[b][:], rstd[:, b, 0:N], ALU.mult).then_inc(S["xn"], 1)
                    nc.vector.scalar_tensor_tensor(out=run[:, b, 0, 1:N + 1], in0=C[b][:], scalar=col("ln1_w"),
                                                   in1=rstd[:, b, N:2 * N], op0=ALU.mult,
                                                   op1=ALU.mult).then_inc(S["ln1"], 1)
                for b in range(B):
                    dve.wait_ge(S["ln1"], at(t, b))
                    nc.vector.tensor_scalar(tsg[:, b, :], run[:, b, 0, 0:N], col("time_shift"), col("ln1_b"),
                                            ALU.mult, ALU.subtract).then_inc(S["tsg"], 1)
                for b in range(B):
                    dve.wait_ge(S["tsg"], at(t, b))
                    nc.vector.scalar_tensor_tensor(out=mix[:, b, :], in0=run[:, b, 0, 1:N + 1], scalar=G.one_p_ts,
                                                   in1=tsg[:, b, :], op0=ALU.mult,
                                                   op1=ALU.subtract).then_inc(S["mixed"], 1)
                for b in range(B):
                    dve.wait_ge(S["projected"], at(t, b))
                    nc.vector.tensor_tensor_scan(run[:, b, 1, 1:N + 1], K[b][:], zeros[:], run[:, b, 1, 0:1],
                                                 ALU.max, ALU.max).then_inc(S["maxima"], 1)
                for b in range(B):
                    dve.wait_ge(S["maxima"], at(t, b))
                    nc.vector.tensor_tensor(xx[:, b, :], K[b][:], run[:, b, 1, 0:N], ALU.subtract).then_inc(S["steps"], 1)
                for b in range(B):
                    dve.wait_ge(S["steps"], at(t, b))
                    nc.vector.tensor_scalar(arg[:, b, 0, :], xx[:, b, :], 0.0, -1.0, ALU.max, ALU.mult)\
                      .then_inc(S["argA"], 1)
                    nc.vector.tensor_scalar(arg[:, b, 1, :], xx[:, b, :], 0.0, None, ALU.min).then_inc(S["argB"], 1)
                for b in range(B):
                    dve.wait_ge(S["factors"], at(t, b))
                    nc.vector.tensor_tensor_scan(run[:, b, 2, 1:N + 1], fac[:, b, 0, :], fac[:, b, 1, :],
                                                 run[:, b, 2, 0:1], ALU.mult, ALU.add).then_inc(S["sums"], 1)
                for b in range(B):
                    dve.wait_ge(S["logsum"], at(t, b))
                    nc.vector.tensor_tensor(dd[:, b, :], lns[:, b, :], xx[:, b, :], ALU.subtract).then_inc(S["dist"], 1)
                for b in range(B):
                    dve.wait_ge(S["dist"], at(t, b))
                    nc.vector.tensor_scalar(arg[:, b, 0, :], dd[:, b, :], 0.0, None, ALU.min).then_inc(S["argC"], 1)
                    nc.vector.tensor_scalar(arg[:, b, 1, :], dd[:, b, :], 0.0, -1.0, ALU.max, ALU.mult)\
                      .then_inc(S["argD"], 1)
                for b in range(B):
                    dve.wait_ge(S["decays"], at(t, b))
                    nc.vector.tensor_tensor(bv[:, b, :], V[b][:], fac[:, b, 1, :], ALU.mult).then_inc(S["bv"], 1)
                for b in range(B):
                    dve.wait_ge(S["bv"], at(t, b))
                    nc.vector.tensor_tensor_scan(run[:, b, 3, 1:N + 1], fac[:, b, 0, :], bv[:, b, :],
                                                 run[:, b, 3, 0:1], ALU.mult, ALU.add).then_inc(S["numer"], 1)
                for b in range(B):
                    dve.wait_ge(S["numer"], at(t, b))
                    nc.vector.tensor_tensor(o[:, b, :], V[b][:], run[:, b, 3, 0:N], ALU.subtract).then_inc(S["diff"], 1)
                for b in range(B):
                    dve.wait_ge(S["diff"], at(t, b))
                    dve.wait_ge(S["vweight"], at(t, b))
                    nc.vector.tensor_tensor(o[:, b, :], o[:, b, :], wv[:, b, :], ALU.mult).then_inc(S["blend"], 1)
                for b in range(B):
                    dve.wait_ge(S["blend"], at(t, b))
                    nc.vector.tensor_tensor(o[:, b, :], o[:, b, :], run[:, b, 3, 0:N], ALU.add).then_inc(S["shift"], 1)
                for b in range(B):
                    dve.wait_ge(S["shift"], at(t, b))
                    nc.vector.tensor_copy(run[:, b, :, 0:1], run[:, b, :, N:N + 1]).then_inc(S["carried"], 1)
                for b in range(B):
                    dve.wait_ge(S["rstd2"], at(t, b))
                    nc.vector.scalar_tensor_tensor(out=G2[:, b, ds(t, 1)], in0=C[b][:], scalar=col("ln2_w"),
                                                   in1=rstd[:, b, 0:N], op0=ALU.mult, op1=ALU.mult)\
                      .then_inc(S["centre_free"], 1)
                dve.wait_ge(S["carried"], t * B + B)
            dve.wait_ge(S["centre_free"], NT * B + B)
            for b in range(B):
                nc.vector.tensor_copy(G2[:, b, 0:1], G2[:, b, T:T + 1])


def phase_ffn(nc, G):
    vec, X, XA, G2, col, ds = G.vec, G.X, G.XA, G.G2, G.col, G.ds
    mem = ExitStack()
    with mem:
        def sb(name, shape, dt=F32):
            return mem.enter_context(nc.sbuf_tensor(name, shape, dt))

        tsg = sb("tsg2", [P, B, N])
        mix = sb("mix2", [P, B, N])
        relu = sb("relu2", [P, 2, N])
        kk = sb("kk2", [P, B, FC, N])
        rc = sb("rc2", [P, B, N])
        z = sb("z2", [P, B, N])
        sq = sb("sq2", [P, B, N])
        lnv = sb("lnv2", [P, B, N])
        rstd = sb("rstd2", [P, B, N])
        scaled = sb("scaled2", [P, B, N])
        silu = sb("silu2", [P, 2, N])
        hA = sb("hA2", [P, B, FC, N])
        hB = kk
        w3c = sb("w3c2", [P, FC, P])
        M = [mem.enter_context(nc.psum_tensor(f"pM2_{b}", [P, N], F32)) for b in range(B)]
        Y = [mem.enter_context(nc.psum_tensor(f"pY2_{b}", [P, N], F32)) for b in range(B)]
        R = [mem.enter_context(nc.psum_tensor(f"pR2_{i}", [P, N], F32)) for i in range(4)]

        names = ("scaled_w3 centred_w3 w3_ready tsg mixed keys relus squares gate_in gate values gated residual "
                 "centredA squaredA varianceA logA rstdA scaledA addedA "
                 "centredB squaredB varianceB logB rstdB normedB "
                 "up silus hidden up1 gelu1 up2 gelu2 down "
                 "squaredC varianceC logC rstdC scaledC addedC").split()
        S = mem.enter_context(semaphores_of_phase(nc, "ffn_", names))
        block = mem.enter_context(nc.Block())

        def at(t, b):
            return t * B + (b + 1)

        def nth(t, b, f):
            return t * (B * FC) + (b * FC + f + 1)

        @block.tensor
        def _(pe):
            pe.wait_ge(G.ffn_loaded, 64)
            pe.wait_ge(S["scaled_w3"], 1)
            for f in range(FC):
                last = nc.tensor.matmul(R[0][:, f * P:(f + 1) * P], G.w3w[:, f * P:(f + 1) * P], G.centre,
                                        start=True, stop=True)
            last.then_inc(S["centred_w3"], 1)
            pe.wait_ge(S["w3_ready"], 1)
            with pe.Fori(0, NT) as t:
                for b in range(B):
                    pe.wait_ge(S["mixed"], at(t, b))
                    for f in range(FC):
                        if b:
                            pe.wait_ge(S["squares"], nth(t, b - 1, f))
                        nc.tensor.matmul(R[f][:], G.attw[:, 4 + f, :], mix[:, b, :], start=True, stop=True)\
                          .then_inc(S["keys"], 1)
                    nc.tensor.matmul(M[b][:], G.attw[:, 3, :], mix[:, b, :], start=True, stop=True)\
                      .then_inc(S["gate_in"], 1)
                for b in range(B):
                    for f in range(FC):
                        pe.wait_ge(S["squares"], nth(t, b, f))
                        last = nc.tensor.matmul(Y[b][:], G.cvw[:, f, :], kk[:, b, f, :], start=f == 0, stop=f == FC - 1)
                    last.then_inc(S["values"], 1)
                for b in range(B):
                    pe.wait_ge(S["residual"], at(t, b))
                    nc.tensor.matmul(M[b][:], G.centre, z[:, b, :], start=True, stop=True).then_inc(S["centredA"], 1)
                for b in range(B):
                    pe.wait_ge(S["squaredA"], at(t, b))
                    nc.tensor.matmul(Y[b][:], G.ones, sq[:, b, :], start=True, stop=True).then_inc(S["varianceA"], 1)
                for b in range(B):
                    pe.wait_ge(S["addedA"], at(t, b))
                    nc.tensor.matmul(M[b][:], G.centre, X[:, b, ds(t)], start=True, stop=True).then_inc(S["centredB"], 1)
                for b in range(B):
                    pe.wait_ge(S["squaredB"], at(t, b))
                    nc.tensor.matmul(Y[b][:], G.ones, sq[:, b, :], start=True, stop=True).then_inc(S["varianceB"], 1)
                for b in range(B):
                    pe.wait_ge(S["normedB"], at(t, b))
                    for f in range(FC):
                        i = b * FC + f
                        if i >= 2:
                            pe.wait_ge(S["hidden"], t * (B * FC) + (i - 1))
                        for w in range(2):
                            last = nc.tensor.matmul(R[2 * (i % 2) + w][:], G.ternw[:, w, f * P:(f + 1) * P],
                                                    z[:, b, :], start=True, stop=True)
                        last.then_inc(S["up"], 1)
                for layer, src, done, ready in ((0, hA, S["gelu1"], S["hidden"]), (1, hB, S["gelu2"], S["gelu1"])):
                    up = (S["up1"], S["up2"])[layer]
                    for b in range(B):
                        pe.wait_ge(ready, nth(t, b, FC - 1))
                        for o in range(FC):
                            i = b * FC + o
                            if i >= FC:
                                pe.wait_ge(done, t * (B * FC) + (i - FC + 1))
                            elif layer == 0:
                                pe.wait_ge(S["hidden"], nth(t, B - 1, FC - 1))
                            else:
                                pe.wait_ge(S["gelu1"], nth(t, B - 1, o))
                            for k in range(FC):
                                last = nc.tensor.matmul(R[o][:], G.hidw[:, layer, k, o * P:(o + 1) * P],
                                                        src[:, b, k, :], start=k == 0, stop=k == FC - 1)
                            last.then_inc(up, 1)
                for b in range(B):
                    pe.wait_ge(S["gelu2"], nth(t, b, FC - 1))
                    for k in range(FC):
                        last = nc.tensor.matmul(M[b][:], w3c[:, k, :], hA[:, b, k, :], start=k == 0, stop=k == FC - 1)
                    last.then_inc(S["down"], 1)
                for b in range(B):
                    pe.wait_ge(S["squaredC"], at(t, b))
                    nc.tensor.matmul(Y[b][:], G.ones, sq[:, b, :], start=True, stop=True).then_inc(S["varianceC"], 1)

        @block.scalar
        def _(act):
            def square(src, done, ready, count):
                act.wait_ge(ready, count)
                nc.scalar.activation(sq[:, b, :], src[:], ACT.Square).then_inc(done, 1)

            def inverse_root(src, variance, log, done, count):
                act.wait_ge(variance, count)
                nc.scalar.activation(lnv[:, b, :], src[:], ACT.Ln, bias=G.eps_c).then_inc(log, 1)
                act.wait_ge(log, count)
                nc.scalar.activation(rstd[:, b, :], lnv[:, b, :], ACT.Exp, scale=-0.5).then_inc(done, 1)

            with act.Fori(0, NT) as t:
                for b in range(B):
                    for f in range(FC):
                        i = b * FC + f
                        act.wait_ge(S["keys"], nth(t, b, f))
                        if i >= 2:
                            act.wait_ge(S["squares"], t * (B * FC) + (i - 1))
                        nc.scalar.activation(relu[:, i % 2, :], R[f][:], ACT.Relu).then_inc(S["relus"], 1)
                for b in range(B):
                    act.wait_ge(S["gate_in"], at(t, b))
                    nc.scalar.activation(rc[:, b, :], M[b][:], ACT.Sigmoid).then_inc(S["gate"], 1)
                act.preload_act_table_set("natural_log_exp_and_others")
                for b in range(B):
                    square(M[b], S["squaredA"], S["centredA"], at(t, b))
                for b in range(B):
                    inverse_root(Y[b], S["varianceA"], S["logA"], S["rstdA"], at(t, b))
                for b in range(B):
                    square(M[b], S["squaredB"], S["centredB"], at(t, b))
                for b in range(B):
                    inverse_root(Y[b], S["varianceB"], S["logB"], S["rstdB"], at(t, b))
                for b in range(B):
                    for f in range(FC):
                        i = b * FC + f
                        act.wait_ge(S["up"], nth(t, b, f))
                        if i >= 2:
                            act.wait_ge(S["hidden"], t * (B * FC) + (i - 1))
                        nc.scalar.activation(silu[:, i % 2, :], R[2 * (i % 2)][:], ACT.Silu,
                                             scale=col("w1_s", f)).then_inc(S["silus"], 1)
                for layer, dst, up, done in ((0, hB, S["up1"], S["gelu1"]), (1, hA, S["up2"], S["gelu2"])):
                    for b in range(B):
                        for o in range(FC):
                            act.wait_ge(up, nth(t, b, o))
                            if layer == 1 and o == 0:
                                act.wait_ge(S["up1"], nth(t, b, FC - 1))
                            nc.scalar.activation(dst[:, b, o, :], R[o][:], ACT.Gelu,
                                                 scale=col(("h1_s", "h2_s")[layer], o)).then_inc(done, 1)
                act.preload_act_table_set("natural_log_exp_and_others")
                for b in range(B):
                    square(M[b], S["squaredC"], S["down"], at(t, b))
                for b in range(B):
                    inverse_root(Y[b], S["varianceC"], S["logC"], S["rstdC"], at(t, b))

        @block.vector
        def _(dve):
            dve.wait_ge(G.ffn_loaded, 64)
            nc.vector.tensor_scalar(G.w3w[:, :], G.w3w[:, :], col("w3_s"), None, ALU.mult).then_inc(S["scaled_w3"], 1)
            dve.wait_ge(S["centred_w3"], 1)
            nc.vector.tensor_copy(w3c[:, :, :].rearrange("p a b -> p (a b)"), R[0][:]).then_inc(S["w3_ready"], 1)

            def scale(src, ready, done, count, dst):
                dve.wait_ge(ready, count)
                nc.vector.tensor_tensor(dst, src[:], rstd[:, b, :], ALU.mult).then_inc(done, 1)

            def add_residual(scaled_, added, count):
                dve.wait_ge(scaled_, count)
                nc.vector.tensor_tensor(X[:, b, ds(t)], X[:, b, ds(t)], scaled[:, b, :], ALU.add).then_inc(added, 1)

            with dve.Fori(0, NT) as t:
                for b in range(B):
                    nc.vector.tensor_scalar(tsg[:, b, :], G2[:, b, ds(t)], col("time_shift"), col("ln2_b"),
                                            ALU.mult, ALU.add).then_inc(S["tsg"], 1)
                for b in range(B):
                    dve.wait_ge(S["tsg"], at(t, b))
                    nc.vector.scalar_tensor_tensor(out=mix[:, b, :], in0=G2[:, b, ds(t, 1)], scalar=G.one_m_ts,
                                                   in1=tsg[:, b, :], op0=ALU.mult, op1=ALU.add).then_inc(S["mixed"], 1)
                for b in range(B):
                    for f in range(FC):
                        i = b * FC + f
                        dve.wait_ge(S["relus"], nth(t, b, f))
                        nc.vector.tensor_tensor(kk[:, b, f, :], R[f][:], relu[:, i % 2, :], ALU.mult)\
                          .then_inc(S["squares"], 1)
                for b in range(B):
                    dve.wait_ge(S["values"], at(t, b))
                    dve.wait_ge(S["gate"], at(t, b))
                    nc.vector.tensor_tensor(rc[:, b, :], Y[b][:], rc[:, b, :], ALU.mult).then_inc(S["gated"], 1)
                for b in range(B):
                    dve.wait_ge(S["gated"], at(t, b))
                    nc.vector.tensor_tensor(z[:, b, :], rc[:, b, :], XA[:, b, ds(t)], ALU.add).then_inc(S["residual"], 1)
                for b in range(B):
                    scale(M[b], S["rstdA"], S["scaledA"], at(t, b), scaled[:, b, :])
                for b in range(B):
                    add_residual(S["scaledA"], S["addedA"], at(t, b))
                for b in range(B):
                    scale(M[b], S["rstdB"], S["normedB"], at(t, b), z[:, b, :])
                for b in range(B):
                    for f in range(FC):
                        i = b * FC + f
                        dve.wait_ge(S["silus"], nth(t, b, f))
                        nc.vector.scalar_tensor_tensor(out=hA[:, b, f, :], in0=R[2 * (i % 2) + 1][:],
                                                       scalar=col("w2_s", f), in1=silu[:, i % 2, :],
                                                       op0=ALU.mult, op1=ALU.mult).then_inc(S["hidden"], 1)
                for b in range(B):
                    scale(M[b], S["rstdC"], S["scaledC"], at(t, b), scaled[:, b, :])
                for b in range(B):
                    add_residual(S["scaledC"], S["addedC"], at(t, b))


def phase_ssm(nc, G):
    vec, X, col, ds = G.vec, G.X, G.col, G.ds
    mem = ExitStack()
    BC = 2 * DST
    LAG = 3
    RING = 3
    with mem:
        def sb(name, shape, dt=F32):
            return mem.enter_context(nc.sbuf_tensor(name, shape, dt))

        negA = sb("negA3", [P, CB, DST])
        wsum = sb("wsum3", [P, CB])
        sq = sb("sq3", [P, B, N])
        lnv = rstd = sq
        xn = sb("xn3", [P, B, N])
        raw = sb("raw3", [P, B, CB, N + TAPS - 1])
        h = sb("h3", [P, B, CB, N])
        sgate = sb("sgate3", [P, B, CB, N])
        tsb = xn[0:DTR, :, :]
        split = sb("split3", [3 * BC, B, N], BF16)
        mid = sb("mid3", [3 * BC, B, N], BF16)
        rest = sq[0:3 * BC, :, :]
        dt = sb("dt3", [P, B, CB, N])
        dtu = sb("dtu3", [P, B, CB, N])
        dA = sb("dA3", [P, RING, CB, N])
        dBu = sb("dBu3", [P, RING, CB, N])
        hs = sb("hs3", [P, RING, CB, N])
        csb = sb("csb3", [P, RING, 1, N])
        prod = sb("prod3", [P, RING, CB, N])
        carry = sb("carry3", [P, B, DST, CB])
        Q = [mem.enter_context(nc.psum_tensor(f"pQ3_{i}", [P, N], F32)) for i in range(8)]

        names = ("logA wsum wmean wcentred carry0 centred squared variance logs rstd normed projected raw_in gates "
                 "conv carried h xproj ts_in split1 rest1 split2 split3 split4 dt_in magnitude expm log1p relu dt dtu "
                 "bcastB bcastC dA c_in dBu scan kept prod acc y ygated "
                 "down squaredC varianceC logC rstdC scaledC addedC").split()
        S = mem.enter_context(semaphores_of_phase(nc, "ssm_", names))
        block = mem.enter_context(nc.Block())

        def at(t, b):
            return t * B + (b + 1)

        def chunk(t, b, c):
            return t * (B * CB) + (b * CB + c + 1)

        def step(t, b, n):
            return t * (B * DST) + (b * DST + n + 1)

        @block.sync
        def _(sp):
            for dst, src in ((G.moe13[:, :, :], G.moe_w13), (G.moe2[:, :, :], G.moe_w2), (G.gatew[:, :], G.gate_w)):
                sp.dma_start(dst, src).then_inc(G.moe_loaded, 16)

        @block.tensor
        def _(pe):
            pe.wait_ge(G.ssm_loaded, 48)

            def accumulate(t, b, n):
                pe.wait_ge(S["prod"], step(t, b, n))
                for c in range(CB):
                    last = nc.tensor.matmul(Q[2 * b + c][:], G.ident, prod[:, (b * DST + n) % RING, c, :],
                                            start=n == 0, stop=n == DST - 1)
                last.then_inc(S["acc"], 1)

            with pe.Fori(0, NT) as t:
                for b in range(B):
                    nc.tensor.matmul(Q[2 * b][:], G.centre, X[:, b, ds(t)], start=True, stop=True)\
                      .then_inc(S["centred"], 1)
                for b in range(B):
                    pe.wait_ge(S["squared"], at(t, b))
                    nc.tensor.matmul(Q[2 * b + 1][:], G.ones, sq[:, b, :], start=True, stop=True)\
                      .then_inc(S["variance"], 1)
                for b in range(B):
                    pe.wait_ge(S["normed"], at(t, b))
                    for m, q in enumerate((2 * b, 2 * b + 1, 4 + 2 * b, 5 + 2 * b)):
                        nc.tensor.matmul(Q[q][:], G.win[:, m * P:(m + 1) * P], xn[:, b, :], start=True, stop=True)\
                          .then_inc(S["projected"], 1)
                for b in range(B):
                    pe.wait_ge(S["h"], chunk(t, b, CB - 1))
                    for q, lo, hi in ((2 * b, 0, DTR), (2 * b + 1, DTR, DTR + 3 * BC)):
                        for c in range(CB):
                            last = nc.tensor.matmul(Q[q][0:hi - lo, :], G.wx[:, c, lo:hi], h[:, b, c, :],
                                                    start=c == 0, stop=c == CB - 1)
                        last.then_inc(S["xproj"], 1)
                for b in range(B):
                    pe.wait_ge(S["ts_in"], at(t, b))
                    for c in range(CB):
                        nc.tensor.matmul(Q[4 + 2 * b + c][:], G.dtw[:, c * P:(c + 1) * P], tsb[:, b, :],
                                         start=True, stop=True).then_inc(S["dt_in"], 1)
                for b in range(B):
                    for n in range(DST):
                        i = b * DST + n
                        if n == 0:
                            pe.wait_ge(S["split3"], at(t, b))
                            pe.wait_ge(S["split4"], at(t, b))
                        if i == 0:
                            pe.wait_ge(S["relu"], chunk(t, B - 1, CB - 1))
                        if i >= 2:
                            pe.wait_ge(S["dBu"], t * (B * DST) + (i - 1))
                        nc.tensor.matmul(Q[4 + i % 2][:], G.sel[:, n, :], split[:, b, :], start=True, stop=True)\
                          .then_inc(S["bcastB"], 1)
                        if i >= 2:
                            pe.wait_ge(S["c_in"], t * (B * DST) + (i - 1))
                        nc.tensor.matmul(Q[6 + i % 2][:], G.sel[:, DST + n, :], split[:, b, :],
                                         start=True, stop=True).then_inc(S["bcastC"], 1)
                        if n >= LAG:
                            accumulate(t, b, n - LAG)
                    for n in range(DST - LAG, DST):
                        accumulate(t, b, n)
                for b in range(B):
                    pe.wait_ge(S["ygated"], at(t, b))
                    for c in range(CB):
                        last = nc.tensor.matmul(Q[2 * b][:], G.wout[:, c, :], dt[:, b, c, :],
                                                start=c == 0, stop=c == CB - 1)
                    last.then_inc(S["down"], 1)
                for b in range(B):
                    pe.wait_ge(S["squaredC"], at(t, b))
                    nc.tensor.matmul(Q[2 * b + 1][:], G.ones, sq[:, b, :], start=True, stop=True)\
                      .then_inc(S["varianceC"], 1)
                pe.wait_ge(S["scaledC"], t * B + B)

        @block.scalar
        def _(act):
            act.preload_act_table_set("natural_log_exp_and_others")
            nc.scalar.activation(negA[:, :, :].rearrange("p c n -> p (c n)"),
                                 vec[:, VECS["A_log"]:VECS["A_log"] + CB * DST], ACT.Exp).then_inc(S["logA"], 1)

            def inverse_root(variance, log, done, count):
                act.wait_ge(variance, count)
                nc.scalar.activation(lnv[:, b, :], Q[2 * b + 1][:], ACT.Ln, bias=G.eps_c).then_inc(log, 1)
                act.wait_ge(log, count)
                nc.scalar.activation(rstd[:, b, :], lnv[:, b, :], ACT.Exp, scale=-0.5).then_inc(done, 1)

            with act.Fori(0, NT) as t:
                for b in range(B):
                    act.wait_ge(S["centred"], at(t, b))
                    nc.scalar.activation(sq[:, b, :], Q[2 * b][:], ACT.Square).then_inc(S["squared"], 1)
                for b in range(B):
                    inverse_root(S["variance"], S["logs"], S["rstd"], at(t, b))
                for b in range(B):
                    for c in range(CB):
                        act.wait_ge(S["projected"], t * (4 * B) + (4 * b + c + 1))
                        nc.scalar.activation(raw[:, b, c, TAPS - 1:TAPS - 1 + N], Q[2 * b + c][:], ACT.Copy)\
                          .then_inc(S["raw_in"], 1)
                for b in range(B):
                    act.wait_ge(S["projected"], t * (4 * B) + (4 * b + 4))
                    for c in range(CB):
                        nc.scalar.activation(sgate[:, b, c, :], Q[4 + 2 * b + c][:], ACT.Silu).then_inc(S["gates"], 1)
                for b in range(B):
                    for c in range(CB):
                        act.wait_ge(S["conv"], t * (B * CB * TAPS) + (b * CB * TAPS + (TAPS - 1) * CB + c + 1))
                        nc.scalar.activation(h[:, b, c, :], h[:, b, c, :], ACT.Silu).then_inc(S["h"], 1)
                act.preload_act_table_set("natural_log_exp_and_others")
                for b in range(B):
                    act.wait_ge(S["xproj"], t * (2 * B) + (2 * b + 1))
                    nc.scalar.activation(tsb[:, b, :], Q[2 * b][0:DTR, :], ACT.Copy).then_inc(S["ts_in"], 1)
                    act.wait_ge(S["xproj"], t * (2 * B) + (2 * b + 2))
                    nc.scalar.activation(split[:, b, :], Q[2 * b + 1][0:3 * BC, :], ACT.Copy).then_inc(S["split1"], 1)
                for b in range(B):
                    for c in range(CB):
                        z, bias = Q[4 + 2 * b + c], col("b_dt", c)
                        act.wait_ge(S["dt_in"], chunk(t, b, c))
                        nc.scalar.activation(dtu[:, b, c, :], z[:], ACT.Abs, bias=bias).then_inc(S["magnitude"], 1)
                        nc.scalar.activation(dt[:, b, c, :], z[:], ACT.Relu, bias=bias).then_inc(S["relu"], 1)
                    for c in range(CB):
                        act.wait_ge(S["magnitude"], chunk(t, b, c))
                        nc.scalar.activation(dtu[:, b, c, :], dtu[:, b, c, :], ACT.Exp, scale=-1.0).then_inc(S["expm"], 1)
                    for c in range(CB):
                        act.wait_ge(S["expm"], chunk(t, b, c))
                        nc.scalar.activation(dtu[:, b, c, :], dtu[:, b, c, :], ACT.Ln, bias=1.0).then_inc(S["log1p"], 1)
                for b in range(B):
                    act.wait_ge(S["dt"], at(t, b))
                    for n in range(DST):
                        i = b * DST + n
                        if i >= RING:
                            act.wait_ge(S["scan"], t * (B * DST) + (i - RING + 1))
                        for c in range(CB):
                            last = nc.scalar.activation(dA[:, (b * DST + n) % RING, c, :], dt[:, b, c, :], ACT.Exp,
                                                        scale=negA[:, c, n:n + 1])
                        last.then_inc(S["dA"], 1)
                        act.wait_ge(S["bcastC"], step(t, b, n))
                        if i >= RING:
                            act.wait_ge(S["prod"], t * (B * DST) + (i - RING + 1))
                        nc.scalar.activation(csb[:, (b * DST + n) % RING, 0, :], Q[6 + i % 2][:], ACT.Copy).then_inc(S["c_in"], 1)
                for b in range(B):
                    act.wait_ge(S["down"], at(t, b))
                    nc.scalar.activation(sq[:, b, :], Q[2 * b][:], ACT.Square).then_inc(S["squaredC"], 1)
                for b in range(B):
                    inverse_root(S["varianceC"], S["logC"], S["rstdC"], at(t, b))

        @block.gpsimd
        def _(pool):
            with pool.Fori(0, NT) as t:
                for b in range(B):
                    for n in range(DST):
                        i = b * DST + n
                        pool.wait_ge(S["scan"], step(t, b, n))
                        pool.wait_ge(S["c_in"], step(t, b, n))
                        if i >= RING:
                            pool.wait_ge(S["acc"], t * (B * DST) + (i - RING + 1))
                        nc.gpsimd.tensor_tensor(prod[:, (b * DST + n) % RING, :, :], hs[:, (b * DST + n) % RING, :, :],
                                                csb[:, (b * DST + n) % RING, :, :].to_broadcast([P, CB, N]), ALU.mult)\
                          .then_inc(S["prod"], 1)

        @block.vector
        def _(dve):
            dve.wait_ge(G.ssm_loaded, 48)
            nc.vector.tensor_reduce(wsum[:, :], G.wout, AX.X, ALU.add).then_inc(S["wsum"], 1)
            dve.wait_ge(S["wsum"], 1)
            nc.vector.tensor_scalar(wsum[:, :], wsum[:, :], 1.0 / P, None, ALU.mult).then_inc(S["wmean"], 1)
            dve.wait_ge(S["wmean"], 1)
            for c in range(CB):
                last = nc.vector.tensor_scalar(G.wout[:, c, :], G.wout[:, c, :], wsum[:, c:c + 1], None, ALU.subtract)
            last.then_inc(S["wcentred"], 1)
            dve.wait_ge(S["logA"], 1)
            nc.vector.tensor_scalar(negA[:, :, :], negA[:, :, :], -1.0, None, ALU.mult).then_inc(S["carry0"], 1)
            nc.vector.memset(carry[:], 0.0).then_inc(S["carry0"], 1)
            nc.vector.memset(raw[:, :, :, 0:TAPS - 1], 0.0).then_inc(S["carry0"], 1)
            dve.wait_ge(S["carry0"], 3)
            with dve.Fori(0, NT) as t:
                for b in range(B):
                    dve.wait_ge(S["rstd"], at(t, b))
                    nc.vector.tensor_tensor(xn[:, b, :], Q[2 * b][:], rstd[:, b, :], ALU.mult).then_inc(S["normed"], 1)
                for b in range(B):
                    for k in range(TAPS):
                        for c in range(CB):
                            if k == 0:
                                dve.wait_ge(S["raw_in"], chunk(t, b, c))
                                nc.vector.tensor_scalar(h[:, b, c, :], raw[:, b, c, 0:N], col("conv_w", c),
                                                        col("conv_b", c), ALU.mult, ALU.add).then_inc(S["conv"], 1)
                            else:
                                dve.wait_ge(S["conv"], t * (B * CB * TAPS) + (b * CB * TAPS + (k - 1) * CB + c + 1))
                                nc.vector.scalar_tensor_tensor(out=h[:, b, c, :], in0=raw[:, b, c, k:k + N],
                                                               scalar=col("conv_w", k * CB + c), in1=h[:, b, c, :],
                                                               op0=ALU.mult, op1=ALU.add).then_inc(S["conv"], 1)
                    dve.wait_ge(S["conv"], t * (B * CB * TAPS) + (b + 1) * CB * TAPS)
                    nc.vector.tensor_copy(raw[:, b, :, 0:TAPS - 1], raw[:, b, :, N:N + TAPS - 1]).then_inc(S["carried"], 1)
                for b in range(B):
                    dve.wait_ge(S["split1"], at(t, b))
                    nc.vector.tensor_tensor(rest[:, b, :], Q[2 * b + 1][0:3 * BC, :], split[:, b, :], ALU.subtract)\
                      .then_inc(S["rest1"], 1)
                for b in range(B):
                    dve.wait_ge(S["rest1"], at(t, b))
                    nc.vector.tensor_copy(mid[:, b, :], rest[:, b, :]).then_inc(S["split2"], 1)
                for b in range(B):
                    dve.wait_ge(S["split2"], at(t, b))
                    nc.vector.tensor_copy(split[BC:2 * BC, b, :], mid[BC:2 * BC, b, :]).then_inc(S["split3"], 1)
                    nc.vector.tensor_tensor(split[2 * BC:3 * BC, b, :], rest[2 * BC:3 * BC, b, :],
                                            mid[2 * BC:3 * BC, b, :], ALU.subtract).then_inc(S["split4"], 1)
                for b in range(B):
                    dve.wait_ge(S["log1p"], chunk(t, b, CB - 1))
                    nc.vector.tensor_tensor(dt[:, b, :, :], dt[:, b, :, :], dtu[:, b, :, :], ALU.add)\
                      .then_inc(S["dt"], 1)
                for b in range(B):
                    dve.wait_ge(S["dt"], at(t, b))
                    nc.vector.tensor_tensor(dtu[:, b, :, :], dt[:, b, :, :], h[:, b, :, :], ALU.mult)\
                      .then_inc(S["dtu"], 1)
                for b in range(B):
                    dve.wait_ge(S["dtu"], at(t, b))

                    def scan(n):
                        i = b * DST + n
                        dve.wait_ge(S["dBu"], step(t, b, n))
                        dve.wait_ge(S["dA"], step(t, b, n))
                        if i >= RING:
                            dve.wait_ge(S["prod"], t * (B * DST) + (i - RING + 1))
                            dve.wait_ge(S["kept"], t * (B * DST) + (i - RING + 1))
                        for c in range(CB):
                            last = nc.vector.tensor_tensor_scan(hs[:, (b * DST + n) % RING, c, :], dA[:, (b * DST + n) % RING, c, :],
                                                                dBu[:, (b * DST + n) % RING, c, :], carry[:, b, n, c:c + 1],
                                                                ALU.mult, ALU.add)
                        last.then_inc(S["scan"], 1)

                    def keep(n):
                        dve.wait_ge(S["scan"], step(t, b, n))
                        nc.vector.tensor_copy(carry[:, b, n, :], hs[:, (b * DST + n) % RING, :, N - 1]).then_inc(S["kept"], 1)

                    for n in range(DST + 1):
                        if n < DST:
                            dve.wait_ge(S["bcastB"], step(t, b, n))
                            nc.vector.tensor_tensor(dBu[:, (b * DST + n) % RING, :, :], dtu[:, b, :, :],
                                                    Q[4 + n % 2][:].unsqueeze(1).to_broadcast([P, CB, N]), ALU.mult)\
                              .then_inc(S["dBu"], 1)
                        if n >= 1:
                            scan(n - 1)
                        if n >= 2:
                            keep(n - 2)
                    keep(DST - 1)
                    dve.wait_ge(S["kept"], step(t, b, DST - 1))
                    dve.wait_ge(S["acc"], step(t, b, DST - 1))
                    for c in range(CB):
                        nc.vector.scalar_tensor_tensor(out=h[:, b, c, :], in0=h[:, b, c, :], scalar=col("D", c),
                                                       in1=Q[2 * b + c][:], op0=ALU.mult, op1=ALU.add)\
                          .then_inc(S["y"], 1)
                    dve.wait_ge(S["y"], chunk(t, b, CB - 1))
                    nc.vector.tensor_tensor(dt[:, b, :, :], h[:, b, :, :], sgate[:, b, :, :], ALU.mult)\
                      .then_inc(S["ygated"], 1)
                for b in range(B):
                    dve.wait_ge(S["rstdC"], at(t, b))
                    nc.vector.tensor_tensor(xn[:, b, :], Q[2 * b][:], rstd[:, b, :], ALU.mult).then_inc(S["scaledC"], 1)
                for b in range(B):
                    dve.wait_ge(S["scaledC"], at(t, b))
                    nc.vector.tensor_tensor(X[:, b, ds(t)], X[:, b, ds(t)], xn[:, b, :], ALU.add).then_inc(S["addedC"], 1)
                dve.wait_ge(S["addedC"], t * B + B)


def tiles(engine, body):
    for b in range(B):
        body(0, b)
    with engine.Fori(1, NT - 1) as t:
        for b in range(B):
            body(t, b)
    for b in range(B):
        body(NT - 1, b)


def is_first(t, b):
    return isinstance(t, int) and t == 0 and b == 0


def is_last(t, b):
    return isinstance(t, int) and t == NT - 1 and b == B - 1


def before(t, b):
    return (t, b - 1) if b else (t - 1, B - 1)


def after(t, b):
    return (t, b + 1) if b < B - 1 else (t + 1, 0)


def wait_past(engine, semaphore, count):
    if not isinstance(count, int) or count > 0:
        engine.wait_ge(semaphore, count)


def phase_moe(nc, G):
    vec, X, ds = G.vec, G.X, G.ds
    mem = ExitStack()
    TC = N // P
    U = E * FC
    RING = 4
    LAG = 3
    with mem:
        def sb(name, shape, dt=F32):
            return mem.enter_context(nc.sbuf_tensor(name, shape, dt))

        wmean = sb("wmean4", [P, U])
        iota = sb("iota4", [P, E])
        sq = sb("sq4", [P, B, N])
        lnv = sb("lnv4", [P, B, N])
        rstd = sb("rstd4", [P, B, N])
        xn = sb("xn4", [P, B, N])
        turn = sb("turn4", [P, 1])
        logits = sb("logits4", [P, B, TC, E])
        best = sb("best4", [P, B, TC, E])
        where = sb("where4", [P, B, TC, E], mybir.dt.uint32)
        wheref = sb("wheref4", [P, B, TC, 2])
        gap = sb("gap4", [P, B, TC])
        half = sb("half4", [P, B, TC])
        share = sb("share4", [P, B, TC, 2])
        pick = sb("pick4", [P, B, 2, TC, E])
        comb = sb("comb4", [P, B, TC, E])
        xs = sb("xs4", [P, 2, N])
        silu = sb("silu4", [P, 2, N])
        hid = sb("hid4", [P, RING, N])
        xn_hi = sb("xn_hi4", [P, B, N], F16)
        xn_lo = sb("xn_lo4", [P, B, N], F16)
        xs_hi = sb("xs_hi4", [P, 2, N], F16)
        xs_lo = sb("xs_lo4", [P, 2, N], F16)
        hid_hi = sb("hid_hi4", [P, RING, N], F16)
        hid_lo = sb("hid_lo4", [P, RING, N], F16)
        w13_hi = sb("w13_hi4", [P, E, 2 * FFN], F16)
        w13_lo = sb("w13_lo4", [P, E, 2 * FFN], F16)
        w2_hi = sb("w2_hi4", [P, U, P], F16)
        w2_lo = sb("w2_lo4", [P, U, P], F16)
        MS = mem.enter_context(nc.psum_tensor("pSpread4", [P, N], F32))
        MP = mem.enter_context(nc.psum_tensor("pPrep4", [P, N], F32))
        Y = [mem.enter_context(nc.psum_tensor(f"pY4_{b}", [P, N], F32)) for b in range(B)]
        R = [mem.enter_context(nc.psum_tensor(f"pR4_{i}", [P, N], F32)) for i in range(4)]

        names = ("iota wsum wmean wcentred w13_high w13_low w2_high w2_low "
                 "centred squared variance logs rstd normed xn_high xn_low scores logits best gap where wheref "
                 "tanh share1 share2 picks comb spread scaled_x xs_high xs_low "
                 "up silus hidden hid_high hid_low down "
                 "squaredC varianceC logC rstdC scaledC addedC stored").split()
        S = mem.enter_context(semaphores_of_phase(nc, "moe_", names))
        block = mem.enter_context(nc.Block())

        def at(t, b):
            return t * B + (b + 1)

        def unit(t, b, i):
            return t * (B * U) + (b * U + i + 1)

        def expert(t, b, e):
            return t * (B * E) + (b * E + e + 1)

        @block.sync
        def _(sp):
            sp.dma_start(iota[:, :], G.iota_c).then_inc(S["iota"], 16)
            with sp.Fori(0, NT) as t:
                for b in range(B):
                    sp.wait_ge(S["addedC"], at(t, b))
                    sp.dma_start(G.outT[:, b, ds(t)], X[:, b, ds(t)]).then_inc(S["stored"], 16)
            sp.wait_ge(S["stored"], NT * B * 16)

        @block.tensor
        def _(pe):
            def product(out, w_hi, w_lo, x_hi, x_lo, start, stop):
                nc.tensor.matmul(out, w_hi, x_hi, start=start, stop=False)
                nc.tensor.matmul(out, w_hi, x_lo, start=False, stop=False)
                return nc.tensor.matmul(out, w_lo, x_hi, start=False, stop=stop)

            def prep(t, b, step):
                if step == 0:
                    wait_past(pe, S["logC"], at(t, b) - 2)
                    nc.tensor.matmul(MP[:], G.centre, X[:, b, ds(t)], start=True, stop=True).then_inc(S["centred"], 1)
                elif step == 1:
                    pe.wait_ge(S["squared"], at(t, b))
                    wait_past(pe, S["scaledC"], at(t, b) - 2)
                    nc.tensor.matmul(Y[b][:], G.ones, sq[:, b, :], start=True, stop=True).then_inc(S["variance"], 1)
                elif step == 2:
                    pe.wait_ge(S["normed"], at(t, b))
                    for j in range(TC):
                        last = nc.tensor.matmul(MP[:, j * E:(j + 1) * E], xn[:, b, j * P:(j + 1) * P], G.gatew[:, :],
                                                start=True, stop=True)
                    last.then_inc(S["scores"], 1)

            def tail(t, b):
                pe.wait_ge(S["squaredC"], at(t, b))
                wait_past(pe, S["logits"], at(t, b) + 1 if not is_last(t, b) else at(t, b))
                nc.tensor.matmul(MP[:], G.ones, sq[:, b, :], start=True, stop=True).then_inc(S["varianceC"], 1)

            def spread(t, b, e):
                if e == 0:
                    pe.wait_ge(S["comb"], at(t, b))
                wait_past(pe, S["scaled_x"], expert(t, b, e) - 1)
                for j in range(TC):
                    last = nc.tensor.matmul(MS[:, j * P:(j + 1) * P],
                                            comb[:, b, j, e:e + 1].to_broadcast([P, P]), G.ident,
                                            start=True, stop=True)
                last.then_inc(S["spread"], 1)

            def down(t, b, i):
                pe.wait_ge(S["hid_low"], unit(t, b, i))
                product(Y[b][:], w2_hi[:, i, :], w2_lo[:, i, :], hid_hi[:, i % RING, :], hid_lo[:, i % RING, :],
                        i == 0, i == U - 1).then_inc(S["down"], 1)

            def body(t, b):
                for i in range(U):
                    e, f = divmod(i, FC)
                    if i == 5 and not is_first(t, b):
                        tail(*before(t, b))
                    if not is_last(t, b) and i in (9, 12, 16):
                        prep(*after(t, b), (9, 12, 16).index(i))
                    if f == 0 and e + 1 < E:
                        spread(t, b, e + 1)
                    elif f == 0 and not is_last(t, b):
                        spread(*after(t, b), 0)
                    if i == 0:
                        pe.wait_ge(S["xn_low"], at(t, b))
                    wait_past(pe, S["hidden"], unit(t, b, i) - 2)
                    m1, m3 = slice(f * P, (f + 1) * P), slice(FFN + f * P, FFN + (f + 1) * P)
                    product(R[2 * (i % 2)][:], w13_hi[:, e, m1], w13_lo[:, e, m1],
                            xn_hi[:, b, :], xn_lo[:, b, :], True, True)
                    if f == 0:
                        pe.wait_ge(S["xs_low"], expert(t, b, e))
                    product(R[2 * (i % 2) + 1][:], w13_hi[:, e, m3], w13_lo[:, e, m3],
                            xs_hi[:, e % 2, :], xs_lo[:, e % 2, :], True, True).then_inc(S["up"], 1)
                    if i >= LAG:
                        down(t, b, i - LAG)
                    elif not is_first(t, b):
                        down(*before(t, b), U - LAG + i)

            pe.wait_ge(G.moe_loaded, 48)
            for step in range(3):
                prep(0, 0, step)
            spread(0, 0, 0)
            pe.wait_ge(S["w13_low"], E)
            pe.wait_ge(S["w2_low"], 1)
            tiles(pe, body)
            for i in range(U - LAG, U):
                down(NT - 1, B - 1, i)
            tail(NT - 1, B - 1)

        @block.scalar
        def _(act):
            def inverse_root(src, variance, log, done, t, b):
                act.preload_act_table_set("natural_log_exp_and_others")
                act.wait_ge(variance, at(t, b))
                nc.scalar.activation(lnv[:, b, :], src[:], ACT.Ln, bias=G.eps_c).then_inc(log, 1)
                act.wait_ge(log, at(t, b))
                nc.scalar.activation(rstd[:, b, :], lnv[:, b, :], ACT.Exp, scale=-0.5).then_inc(done, 1)

            def prep(t, b, step):
                if step == 0:
                    act.wait_ge(S["centred"], at(t, b))
                    nc.scalar.activation(sq[:, b, :], MP[:], ACT.Square).then_inc(S["squared"], 1)
                elif step == 1:
                    inverse_root(Y[b], S["variance"], S["logs"], S["rstd"], t, b)
                elif step == 2:
                    act.wait_ge(S["normed"], at(t, b))
                    nc.scalar.activation(xn_hi[:, b, :], xn[:, b, :], ACT.Copy).then_inc(S["xn_high"], 1)
                elif step == 3:
                    act.wait_ge(S["gap"], at(t, b))
                    nc.scalar.activation(half[:, b, :], gap[:, b, :], ACT.Tanh, scale=0.5).then_inc(S["tanh"], 1)

            def tail(t, b, step):
                if step == 0:
                    act.wait_ge(S["down"], unit(t, b, U - 1))
                    nc.scalar.activation(sq[:, b, :], Y[b][:], ACT.Square, scale=1.0 / WS).then_inc(S["squaredC"], 1)
                elif step == 1:
                    inverse_root(MP, S["varianceC"], S["logC"], S["rstdC"], t, b)

            def hid_high(t, b, i):
                act.wait_ge(S["hidden"], unit(t, b, i))
                nc.scalar.activation(hid_hi[:, i % RING, :], hid[:, i % RING, :], ACT.Copy).then_inc(S["hid_high"], 1)

            def body(t, b):
                for i in range(U):
                    act.wait_ge(S["up"], unit(t, b, i))
                    nc.scalar.activation(silu[:, i % 2, :], R[2 * (i % 2)][:], ACT.Silu,
                                         scale=1.0 / WS).then_inc(S["silus"], 1)
                    if i >= 1:
                        hid_high(t, b, i - 1)
                    if not is_first(t, b) and i in (3, 6):
                        tail(*before(t, b), (3, 6).index(i))
                    if not is_last(t, b) and i in (9, 12, 14, 20):
                        prep(*after(t, b), (9, 12, 14, 20).index(i))
                hid_high(t, b, U - 1)

            for step in range(2):
                prep(0, 0, step)
            act.wait_ge(G.moe_loaded, 48)
            for e in range(E):
                nc.scalar.activation(w13_hi[:, e, :], G.moe13[:, e, :], ACT.Copy, scale=WS).then_inc(S["w13_high"], 1)
            act.wait_ge(S["wcentred"], 1)
            nc.scalar.activation(w2_hi[:, :, :], G.moe2[:, :, :], ACT.Copy, scale=WS).then_inc(S["w2_high"], 1)
            for step in range(2, 4):
                prep(0, 0, step)
            tiles(act, body)
            for step in range(2):
                tail(NT - 1, B - 1, step)

        @block.gpsimd
        def _(pool):
            def prep(t, b):
                pool.wait_ge(S["xn_high"], at(t, b))
                nc.gpsimd.tensor_tensor(xn_lo[:, b, :], xn[:, b, :], xn_hi[:, b, :], ALU.subtract)\
                  .then_inc(S["xn_low"], 1)

            def body(t, b):
                for i in range(U):
                    pool.wait_ge(S["hid_high"], unit(t, b, i))
                    nc.gpsimd.tensor_tensor(hid_lo[:, i % RING, :], hid[:, i % RING, :], hid_hi[:, i % RING, :],
                                            ALU.subtract).then_inc(S["hid_low"], 1)
                    if i == 15 and not is_last(t, b):
                        prep(*after(t, b))

            prep(0, 0)
            tiles(pool, body)

        @block.vector
        def _(dve):
            gate_b = vec[:, VECS["gate_b"]:VECS["gate_b"] + E].unsqueeze(1).to_broadcast([P, TC, E])

            def prep(t, b, step):
                if step == 0:
                    wait_past(dve, S["addedC"], at(t, b) - 2)
                    dve.wait_ge(S["rstd"], at(t, b))
                    nc.vector.tensor_tensor(xn[:, b, :], MP[:], rstd[:, b, :], ALU.mult).then_inc(S["normed"], 1)
                elif step == 1:
                    dve.wait_ge(S["scores"], at(t, b))
                    nc.vector.tensor_tensor(logits[:, b, :, :], MP[:, 0:TC * E].rearrange("p (j e) -> p j e", j=TC),
                                            gate_b, ALU.add).then_inc(S["logits"], 1)
                elif step == 2:
                    dve.wait_ge(S["logits"], at(t, b))
                    nc.vector.memset(turn[:, :], 0.0)
                    for j in range(TC):
                        last = nc.vector.max(best[:, b, j, :], logits[:, b, j, :])
                    last.then_inc(S["best"], 1)
                elif step == 3:
                    dve.wait_ge(S["best"], at(t, b))
                    nc.vector.tensor_tensor(gap[:, b, :], best[:, b, :, 1], best[:, b, :, 0], ALU.subtract)\
                      .then_inc(S["gap"], 1)
                    for j in range(TC):
                        last = nc.vector.max_index(where[:, b, j, :], best[:, b, j, :], logits[:, b, j, :])
                    last.then_inc(S["where"], 1)
                elif step == 4:
                    dve.wait_ge(S["where"], at(t, b))
                    nc.vector.tensor_copy(wheref[:, b, :, :], where[:, b, :, 0:2]).then_inc(S["wheref"], 1)
                    dve.wait_ge(S["tanh"], at(t, b))
                    nc.vector.tensor_scalar(share[:, b, :, 0], half[:, b, :], -0.5, 0.5, ALU.mult, ALU.add)\
                      .then_inc(S["share1"], 1)
                    nc.vector.tensor_scalar(share[:, b, :, 1], half[:, b, :], 0.5, 0.5, ALU.mult, ALU.add)\
                      .then_inc(S["share2"], 1)
                elif step == 5:
                    dve.wait_ge(S["share1"], at(t, b))
                    dve.wait_ge(S["share2"], at(t, b))
                    dve.wait_ge(S["wheref"], at(t, b))
                    for r in range(2):
                        for j in range(TC):
                            last = nc.vector.tensor_scalar(pick[:, b, r, j, :], iota[:, :], wheref[:, b, j, r:r + 1],
                                                           share[:, b, j, r:r + 1], ALU.is_equal, ALU.mult)
                    last.then_inc(S["picks"], 1)
                elif step == 6:
                    dve.wait_ge(S["picks"], at(t, b))
                    nc.vector.tensor_tensor(comb[:, b, :, :], pick[:, b, 0, :, :], pick[:, b, 1, :, :], ALU.add)\
                      .then_inc(S["comb"], 1)

            def tail(t, b, step):
                if step == 0:
                    dve.wait_ge(S["rstdC"], at(t, b))
                    nc.vector.scalar_tensor_tensor(out=xn[:, b, :], in0=Y[b][:], scalar=1.0 / WS, in1=rstd[:, b, :],
                                                   op0=ALU.mult, op1=ALU.mult).then_inc(S["scaledC"], 1)
                elif step == 1:
                    dve.wait_ge(S["scaledC"], at(t, b))
                    nc.vector.tensor_tensor(X[:, b, ds(t)], X[:, b, ds(t)], xn[:, b, :], ALU.add)\
                      .then_inc(S["addedC"], 1)

            def scaled_input(t, b, e, step):
                if step == 0:
                    dve.wait_ge(S["spread"], expert(t, b, e))
                    wait_past(dve, S["xs_low"], expert(t, b, e) - 2)
                    nc.vector.tensor_tensor(xs[:, e % 2, :], xn[:, b, :], MS[:], ALU.mult).then_inc(S["scaled_x"], 1)
                elif step == 1:
                    dve.wait_ge(S["scaled_x"], expert(t, b, e))
                    wait_past(dve, S["up"], unit(t, b, 0) - 1 + (e - 1) * FC)
                    nc.vector.tensor_copy(xs_hi[:, e % 2, :], xs[:, e % 2, :]).then_inc(S["xs_high"], 1)
                elif step == 2:
                    dve.wait_ge(S["xs_high"], expert(t, b, e))
                    nc.vector.tensor_tensor(xs_lo[:, e % 2, :], xs[:, e % 2, :], xs_hi[:, e % 2, :], ALU.subtract)\
                      .then_inc(S["xs_low"], 1)

            def body(t, b):
                for i in range(U):
                    e, f = divmod(i, FC)
                    dve.wait_ge(S["silus"], unit(t, b, i))
                    wait_past(dve, S["down"], unit(t, b, i) - RING)
                    nc.vector.scalar_tensor_tensor(out=hid[:, i % RING, :], in0=R[2 * (i % 2) + 1][:],
                                                   scalar=1.0 / WS, in1=silu[:, i % 2, :], op0=ALU.mult,
                                                   op1=ALU.mult).then_inc(S["hidden"], 1)
                    if f < 3 and e + 1 < E:
                        scaled_input(t, b, e + 1, f)
                    elif f < 3 and not is_last(t, b):
                        scaled_input(*after(t, b), 0, f)
                    if not is_first(t, b) and i in (7, 8):
                        tail(*before(t, b), (7, 8).index(i))
                    if not is_last(t, b) and i in (13, 16, 17, 18, 20, 21, 22):
                        prep(*after(t, b), (13, 16, 17, 18, 20, 21, 22).index(i))

            dve.wait_ge(S["iota"], 16)
            prep(0, 0, 0)
            dve.wait_ge(G.moe_loaded, 48)
            nc.vector.tensor_reduce(wmean[:, :], G.moe2[:, :, :], AX.X, ALU.add).then_inc(S["wsum"], 1)
            dve.wait_ge(S["wsum"], 1)
            nc.vector.tensor_scalar(wmean[:, :], wmean[:, :], 1.0 / P, None, ALU.mult).then_inc(S["wmean"], 1)
            dve.wait_ge(S["wmean"], 1)
            nc.vector.tensor_tensor(G.moe2[:, :, :], G.moe2[:, :, :], wmean[:, :].unsqueeze(2).to_broadcast([P, U, P]),
                                    ALU.subtract).then_inc(S["wcentred"], 1)
            for e in range(E):
                dve.wait_ge(S["w13_high"], e + 1)
                nc.vector.scalar_tensor_tensor(out=w13_lo[:, e, :], in0=G.moe13[:, e, :], scalar=WS,
                                               in1=w13_hi[:, e, :], op0=ALU.mult, op1=ALU.subtract)\
                  .then_inc(S["w13_low"], 1)
            dve.wait_ge(S["w2_high"], 1)
            nc.vector.scalar_tensor_tensor(out=w2_lo[:, :, :], in0=G.moe2[:, :, :], scalar=WS, in1=w2_hi[:, :, :],
                                           op0=ALU.mult, op1=ALU.subtract).then_inc(S["w2_low"], 1)
            for step in range(1, 7):
                prep(0, 0, step)
            for step in range(3):
                scaled_input(0, 0, 0, step)
            tiles(dve, body)
            for step in range(2):
                tail(NT - 1, B - 1, step)


def kernel(**inputs):
    import numpy as np
    import concourse.bacc as bacc
    from concourse.bass_utils import run_bass_kernel_spmd

    a = {k: np.asarray(v) for k, v in inputs.items()}

    def chunks(v):
        return v.reshape(-1, P).T

    def rows(w):
        return w.reshape(-1, P, w.shape[-1]).transpose(1, 0, 2)

    L0, L1, F0, F1 = "L0_attn_", "L1_attn_", "L0_ffn_", "L1_ffn_"
    vecs = np.concatenate([
        a[L0 + "time_first"][:, None], a[L0 + "time_shift"].reshape(P, 1), a[L0 + "ln1_w"][:, None],
        a[L0 + "ln1_b"][:, None], a[L0 + "ln2_w"][:, None], a[L0 + "ln2_b"][:, None],
        chunks(a[F0 + "w1_s"]), chunks(a[F0 + "w2_s"]), chunks(a[F0 + "h1_s"]), chunks(a[F0 + "h2_s"]),
        chunks(a[F0 + "w3_s"]),
        a[L1 + "conv_w"].reshape(TAPS, CB, P).transpose(2, 0, 1).reshape(P, TAPS * CB),
        chunks(a[L1 + "conv_b"]), chunks(a[L1 + "b_dt"]), chunks(a[L1 + "D"]),
        rows(a[L1 + "A_log"]).reshape(P, CB * DST), np.broadcast_to(a[F1 + "gate_b"], (P, E)),
    ], axis=1)
    wxs = a[L1 + "W_x"]
    wxs = np.concatenate([wxs[:, 0:DTR]] + [wxs[:, DTR:]] * 3, axis=1)
    selectors = np.zeros((3 * 2 * DST, 2 * DST, P), np.float32)
    for n in range(2 * DST):
        selectors[n::2 * DST, n, :] = 1.0
    bf16 = np.dtype("bfloat16")
    arrays = {
        "xT": a[L0 + "x"].transpose(2, 0, 1),
        "vecs": vecs,
        "att_w": np.concatenate([a[L0 + w].T for w in ("Wk", "Wv", "Wr", "Wcr", "Wck")], axis=1).reshape(P, 8, P),
        "cv_w": rows(a[L0 + "Wcv"].T),
        "tern_w": np.stack([a[F0 + "w1_w"].T, a[F0 + "w2_w"].T], axis=1),
        "hid_w": np.stack([rows(a[F0 + "h1_w"].T), rows(a[F0 + "h2_w"].T)], axis=1),
        "w3_w": a[F0 + "w3_w"],
        "ssm_w": np.concatenate([a[L1 + "W_in"], rows(wxs).reshape(P, -1), rows(a[L1 + "W_out"]).reshape(P, -1)],
                                axis=1),
        "dt_w": a[L1 + "W_dt"],
        "moe_w13": np.concatenate([a[F1 + "w1"], a[F1 + "w3"]], axis=2).transpose(1, 0, 2),
        "moe_w2": rows(a[F1 + "w2"].reshape(E * FFN, P)),
        "gate_w": a[F1 + "gate_w"],
        "consts": np.stack([np.eye(P), np.eye(P) - 1.0 / P, np.full((P, P), 1.0 / P)], axis=1).astype(np.float32),
        "selectors": selectors.astype(bf16),
        "iota_c": np.broadcast_to(np.arange(E, dtype=np.float32), (P, E)),
    }
    nc = bacc.Bacc("TRN2", target_bir_lowering=False, num_devices=1)
    args = {}
    for name, value in arrays.items():
        arrays[name] = value = np.ascontiguousarray(value)
        args[name] = nc.dram_tensor(name, value.shape, mybir.dt.from_np(value.dtype), kind="ExternalInput").ap()
    outT = nc.dram_tensor("outT", (P, B, T), F32, kind="ExternalOutput").ap()
    build(nc, outT=outT, **args)
    r = run_bass_kernel_spmd(nc, [arrays], core_ids=[0])
    return np.ascontiguousarray(r.results[0]["outT"].transpose(1, 2, 0))
```
